# Optimizing a Trainium2 kernel written in Bass

```python
import numpy as np
import jax
import jax.numpy as jnp

def _softmax(x, axis=-1):
    return jax.nn.softmax(x, axis=axis)

def _gelu(x):
    return jax.nn.gelu(x, approximate=True)

def _silu(x):
    return jax.nn.silu(x)

def _sigmoid(x):
    return jax.nn.sigmoid(x)

def _layernorm(x, axis=-1, eps=1e-05):
    m = jnp.mean(x, axis=axis, keepdims=True)
    v = jnp.var(x, axis=axis, keepdims=True)
    return (x - m) / jnp.sqrt(v + eps)

def _scatter_add(tgt, idx, src, axis=0):
    return tgt.at[idx].add(src)

def _segment_sum(src, seg, n):
    return jax.ops.segment_sum(src, seg, n)
kernel_name = 'mk_gnn_resnorm_d2_gnn_r8_e47116'

def setup_inputs(seed: int=0):
    np.random.seed(seed)
    _w = jnp.asarray

    def _rec_inputs():
        import jax
        import jax.numpy as jnp
        _gk = jax.random.key(seed)
        x = -0.0001006 + 1 * jax.random.normal(jax.random.fold_in(_gk, 1), (6250, 96), jnp.float32)
        src = jax.random.randint(jax.random.fold_in(_gk, 2), (100000,), 0, 6250, jnp.int32)
        dst = jax.random.randint(jax.random.fold_in(_gk, 3), (100000,), 0, 6250, jnp.int32)
        _o = jnp.argsort(dst, stable=True)
        src = src[_o]
        dst = dst[_o]
        edge_attr_32 = 0.000196303 + 1.00016 * jax.random.normal(jax.random.fold_in(_gk, 11), (100000, 32), jnp.float32)
        edge_weight = jax.random.uniform(jax.random.fold_in(_gk, 13), (100000,), jnp.float32, 0.0, 1)
        return (x, src, dst, edge_attr_32, edge_weight)
    x, src, dst, edge_attr_32, edge_weight = _rec_inputs()

    def _L0_gnn_setup():
        import jax, jax.numpy as jnp
        import numpy as np
        N, E = (6250, 100000)
        ND, ED = (96, 32)

        def _gelu(x):
            return jax.nn.gelu(x, approximate=False)
        key = jax.random.key(seed)
        ks = jax.random.split(key, 16)
        s = lambda fan_in: 1.0 / np.sqrt(fan_in)
        inp = {'x': jax.random.normal(ks[0], (N, ND), jnp.float32), 'edge_index': jax.random.randint(ks[1], (2, E), 0, N, jnp.int32), 'edge_attr': jax.random.normal(ks[2], (E, ED), jnp.float32), 'mW1': jax.random.uniform(ks[3], (ND + ED, ND), jnp.float32, -s(ND + ED), s(ND + ED)), 'mb1': jnp.zeros((ND,), jnp.float32), 'mW2': jax.random.uniform(ks[4], (ND, ND), jnp.float32, -s(ND), s(ND)), 'mb2': jnp.zeros((ND,), jnp.float32), 'gW1': jax.random.uniform(ks[5], (ND + ED, ND), jnp.float32, -s(ND + ED), s(ND + ED)), 'gb1': jnp.zeros((ND,), jnp.float32), 'gW2': jax.random.uniform(ks[6], (ND, 1), jnp.float32, -s(ND), s(ND)), 'gb2': jnp.zeros((1,), jnp.float32), 'uW1': jax.random.uniform(ks[7], (2 * ND, ND), jnp.float32, -s(2 * ND), s(2 * ND)), 'ub1': jnp.zeros((ND,), jnp.float32), 'uW2': jax.random.uniform(ks[8], (ND, ND), jnp.float32, -s(ND), s(ND)), 'ub2': jnp.zeros((ND,), jnp.float32), 'ln_g': jnp.ones((ND,), jnp.float32), 'ln_b': jnp.zeros((ND,), jnp.float32)}
        return inp
    _L0_gnn_all = _L0_gnn_setup()
    _L0_gnn_in = {k: v for k, v in _L0_gnn_all.items() if k in ('mW1', 'mb1', 'mW2', 'mb2', 'gW1', 'gb1', 'gW2', 'gb2', 'uW1', 'ub1', 'uW2', 'ub2', 'ln_g', 'ln_b')}
    del _L0_gnn_all

    def _L1_gnn_setup():
        import jax, jax.numpy as jnp
        import numpy as np
        N_NODES = 6250
        N_EDGES = 100000
        D_IN = 96
        D_OUT = 96
        key = jax.random.key(seed)
        k1, k2, k3 = jax.random.split(key, 3)
        x = jax.random.normal(k1, (N_NODES, D_IN), dtype=jnp.float32)
        edge_index = jax.random.randint(k2, (2, N_EDGES), 0, N_NODES, dtype=jnp.int64)
        edge_weight = jnp.ones((N_EDGES,), dtype=jnp.float32)
        W = jax.random.normal(k3, (D_IN, D_OUT), dtype=jnp.float32) * (1.0 / np.sqrt(D_IN))
        b = jnp.zeros((D_OUT,), dtype=jnp.float32)
        return {'x': x, 'edge_index': edge_index, 'edge_weight': edge_weight, 'W': W, 'b': b}
    _L1_gnn_all = _L1_gnn_setup()
    _L1_gnn_in = {k: v for k, v in _L1_gnn_all.items() if k in ('W', 'b')}
    del _L1_gnn_all
    return {'x': x, 'src': src, 'dst': dst, 'edge_attr_32': edge_attr_32, 'edge_weight': edge_weight, 'L0_gnn_mW1': _L0_gnn_in['mW1'], 'L0_gnn_mb1': _L0_gnn_in['mb1'], 'L0_gnn_mW2': _L0_gnn_in['mW2'], 'L0_gnn_mb2': _L0_gnn_in['mb2'], 'L0_gnn_gW1': _L0_gnn_in['gW1'], 'L0_gnn_gb1': _L0_gnn_in['gb1'], 'L0_gnn_gW2': _L0_gnn_in['gW2'], 'L0_gnn_gb2': _L0_gnn_in['gb2'], 'L0_gnn_uW1': _L0_gnn_in['uW1'], 'L0_gnn_ub1': _L0_gnn_in['ub1'], 'L0_gnn_uW2': _L0_gnn_in['uW2'], 'L0_gnn_ub2': _L0_gnn_in['ub2'], 'L0_gnn_ln_g': _L0_gnn_in['ln_g'], 'L0_gnn_ln_b': _L0_gnn_in['ln_b'], 'L1_gnn_W': _L1_gnn_in['W'], 'L1_gnn_b': _L1_gnn_in['b']}

def reference(x, src, dst, edge_attr_32, edge_weight, L0_gnn_mW1, L0_gnn_mb1, L0_gnn_mW2, L0_gnn_mb2, L0_gnn_gW1, L0_gnn_gb1, L0_gnn_gW2, L0_gnn_gb2, L0_gnn_uW1, L0_gnn_ub1, L0_gnn_uW2, L0_gnn_ub2, L0_gnn_ln_g, L0_gnn_ln_b, L1_gnn_W, L1_gnn_b):
    import jax
    import jax.numpy as jnp

    def _L0_gnn_ref(x, edge_index, edge_attr, mW1, mb1, mW2, mb2, gW1, gb1, gW2, gb2, uW1, ub1, uW2, ub2, ln_g, ln_b):
        import jax, jax.numpy as jnp
        import numpy as np
        N, E = (6250, 100000)
        ND, ED = (96, 32)

        def _gelu(x):
            return jax.nn.gelu(x, approximate=False)
        src, dst = (edge_index[0], edge_index[1])
        edge_input = jnp.concatenate([x[src], edge_attr], axis=-1)
        messages = _gelu(edge_input @ mW1 + mb1) @ mW2 + mb2
        gates = jax.nn.sigmoid(_gelu(edge_input @ gW1 + gb1) @ gW2 + gb2)
        aggregated = jax.ops.segment_sum(messages * gates, dst, num_segments=x.shape[0])
        combined = jnp.concatenate([x, aggregated], axis=-1)
        update = _gelu(combined @ uW1 + ub1) @ uW2 + ub2
        h = x + update
        mu = jnp.mean(h, axis=-1, keepdims=True)
        var = jnp.mean(jnp.square(h - mu), axis=-1, keepdims=True)
        return (h - mu) * jax.lax.rsqrt(var + 1e-05) * ln_g + ln_b

    def _L1_gnn_ref(x, edge_index, edge_weight, W, b):
        import jax, jax.numpy as jnp
        import numpy as np
        N_NODES = 6250
        N_EDGES = 100000
        D_IN = 96
        D_OUT = 96
        'PyG GCNConv: out = D^{-1/2} (A + I) D^{-1/2} (x @ W) + b.'
        N = x.shape[0]
        row, col = (edge_index[0], edge_index[1])
        loop = jnp.arange(N, dtype=edge_index.dtype)
        row = jnp.concatenate([row, loop])
        col = jnp.concatenate([col, loop])
        ew = jnp.concatenate([edge_weight, jnp.ones((N,), dtype=edge_weight.dtype)])
        deg = jax.ops.segment_sum(ew, col, num_segments=N)
        dinv = jnp.where(deg > 0, jax.lax.rsqrt(deg), 0.0)
        norm = dinv[row] * ew * dinv[col]
        h = x @ W
        msg = h[row] * norm[:, None]
        out = jax.ops.segment_sum(msg, col, num_segments=N)
        return out + b
    edge_index = jnp.stack([src, dst])
    x = _layernorm(x + _L0_gnn_ref(x, edge_index, edge_attr_32, L0_gnn_mW1, L0_gnn_mb1, L0_gnn_mW2, L0_gnn_mb2, L0_gnn_gW1, L0_gnn_gb1, L0_gnn_gW2, L0_gnn_gb2, L0_gnn_uW1, L0_gnn_ub1, L0_gnn_uW2, L0_gnn_ub2, L0_gnn_ln_g, L0_gnn_ln_b), axis=-1)
    x = _layernorm(x + _L1_gnn_ref(x, edge_index, edge_weight, L1_gnn_W, L1_gnn_b), axis=-1)
    return x

_drawn_inputs = setup_inputs


def setup_inputs(seed=0):
    import zlib

    import numpy as np

    out = dict(_drawn_inputs(seed))
    spreads = {'L0_gnn_mb1': (0.0, 0.428),
     'L0_gnn_mb2': (0.0, 0.1),
     'L0_gnn_gb1': (0.0, 2.0),
     'L0_gnn_ub1': (0.0, 0.314),
     'L0_gnn_ub2': (0.0, 0.1),
     'L0_gnn_ln_g': (1.0, 0.2),
     'L0_gnn_ln_b': (0.0, 0.1),
     'L1_gnn_b': (0.0, 0.1)}
    factors = {'edge_attr_32': 3.863, 'L0_gnn_gW1': 8.0, 'L0_gnn_gW2': 8.0}
    for name, (base, spread) in spreads.items():
        noise = np.random.default_rng([zlib.crc32(name.encode()), seed]).standard_normal(out[name].shape)
        drawn = base * np.exp(spread * noise) if base else spread * noise
        out[name] = jnp.asarray(drawn.astype(out[name].dtype))
    for name, factor in factors.items():
        out[name] = (out[name] * factor).astype(out[name].dtype)
    return out
```

```python
import concourse.bass as bass
from concourse import mybir
from contextlib import ExitStack

P = 128
N, E = 6250, 100000
ND, ED = 96, 32
TG = 8
GE = TG * P
NG = -(-E // GE)
NG += NG % 2
TURNS = NG // 2
NT = NG * TG
W = 80
BR = 5
RN = BR * P
NR = -(-N // RN)
NR += NR % 2
NP = NR * RN
NW = -(-NP // W)
AW = NP + 2 * W
VC = ND + 2
HC = 2 * ND
RH = RN // 2
EPS = 1e-5


def gnn_kernel(nc, t, out):
    fp32, i32 = mybir.dt.float32, mybir.dt.int32
    ALU = mybir.AluOpType
    ACT = mybir.ActivationFunctionType
    AX = mybir.AxisListType.X
    ds = bass.ds

    hidden_table = nc.dram_tensor("hidden_table", [NP, HC], fp32, kind="Internal").ap()
    x1s_table = nc.dram_tensor("x1s_table", [NP, ND], fp32, kind="Internal").ap()

    ctx = ExitStack()
    with ctx:
        def sb(name, shape, dt=fp32):
            return ctx.enter_context(nc.sbuf_tensor(name, shape, dt))

        def sem(name):
            return ctx.enter_context(nc.semaphore(name))

        ident = sb("ident", [P, P])
        before = sb("before", [P, NG])
        ones = sb("ones", [P, P])
        iota_w = sb("iota_w", [P, W])
        iota_i = sb("iota_i", [P, W], i32)
        win_i = sb("win_i", [P, NW], i32)
        win_off = sb("win_off", [P, NW])
        pick_w = sb("pick_w", [P, 1])
        w1x = sb("w1x", [ND + 1, HC])
        w1e = sb("w1e", [P, HC])
        gw2 = sb("gw2", [P, ND])
        gb2 = sb("gb2", [P, 1])
        half_gb2 = sb("half_gb2", [P, 1])
        mw2 = sb("mw2", [ND + 1, ND])
        uw1x = sb("uw1x", [ND + 1, ND])
        uw1a = sb("uw1a", [ND, ND])
        uw2 = sb("uw2", [ND + 1, ND])
        w_gcn = sb("w_gcn", [ND, ND])
        ln_g = sb("ln_g", [P, ND])
        ln_b = sb("ln_b", [P, ND])
        b_gcn = sb("b_gcn", [P, ND])
        minus_half = sb("minus_half", [P, BR])
        dst_rows = sb("dst_rows", [NG, GE], i32)
        lo = sb("lo", [NG, 1])
        hi = sb("hi", [NG, 1])
        reach = sb("reach", [NG, 1])
        crossed = sb("crossed", [NG, NW])
        extra = sb("extra", [NG, 1])
        spread = sb("spread", [NG, 3, NG])
        lo_all = sb("lo_all", [P, NG])
        steer = sb("steer", [1, 3, NG], i32)
        dst_i = sb("dst_i", [P, NT], i32)
        dst_rel = sb("dst_rel", [P, NT])
        weight = sb("weight", [P, NT])
        x_t = sb("x_t", [ND + 1, NP])
        x_nat = sb("x_nat", [P, NR * BR, ND])
        x1 = sb("x1", [P, NR * BR, ND])
        dinv = sb("dinv", [P, NR * BR])
        acc1 = sb("acc1", [VC, AW])
        acc2 = sb("acc2", [ND, AW])
        idx = [sb(f"idx{u}", [P, TG], i32) for u in range(2)]
        edge_t = [sb(f"edge_t{u}", [P, 2 * P]) for u in range(2)]
        rows = [sb(f"rows{u}", [P, TG, HC]) for u in range(2)]
        hid = [sb(f"hid{u}", [P, TG, HC]) for u in range(2)]
        vals = [sb(f"vals{u}", [P, TG, VC]) for u in range(2)]
        hot = [sb(f"hot{u}", [P, TG, W]) for u in range(2)]
        logit = [sb(f"logit{u}", [P, TG]) for u in range(2)]
        squash = [sb(f"squash{u}", [P, TG]) for u in range(2)]
        prod = sb("prod", [P, TG, ND])
        far_rel = sb("far_rel", [P, TG])
        far_hot = sb("far_hot", [P, TG, W])
        x_blk = [sb(f"x_blk{u}", [ND + 1, RN]) for u in range(2)]
        agg_t = [b[0:ND, :] for b in x_blk]
        upd_t = [sb(f"upd_t{u}", [ND + 1, RN]) for u in range(2)]
        wsum = [sb(f"wsum{u}", [P, RN]) for u in range(2)]
        hn = [sb(f"hn{u}", [P, BR, ND]) for u in range(2)]
        xs = [sb(f"xs{u}", [P, BR, ND]) for u in range(2)]
        stats = sb("stats", [P, BR, 6])
        mv = sb("mv", [P, BR, 2])
        vare = sb("vare", [P, BR])
        rstd = sb("rstd", [P, BR])
        degs = sb("degs", [P, BR])
        degm = sb("degm", [P, BR])
        degp = sb("degp", [P, BR])

        bank = [ctx.enter_context(nc.psum_tensor(f"bank{k}", [P, 512], fp32)) for k in range(8)]

        s_wts = sem("s_wts")
        s_dst = sem("s_dst")
        s_const = sem("s_const")
        s_zero = sem("s_zero")
        s_chain = sem("s_chain")
        s_spread = sem("s_spread")
        s_bcast = sem("s_bcast")
        s_steer = sem("s_steer")
        s_xblk = [sem(f"s_xblk{u}") for u in range(2)]
        s_tab_mm = sem("s_tab_mm")
        s_tab_a = sem("s_tab_a")
        s_tab_w = [sem(f"s_tab_w{u}") for u in range(2)]
        s_idx = [sem(f"s_idx{u}") for u in range(2)]
        s_edge = [sem(f"s_edge{u}") for u in range(2)]
        s_rows = [sem(f"s_rows{u}") for u in range(2)]
        s_pre = sem("s_pre")
        s_sum = sem("s_sum")
        s_hid = [sem(f"s_hid{u}") for u in range(2)]
        s_logit = sem("s_logit")
        s_squash = sem("s_squash")
        s_vals = sem("s_vals")
        s_win = sem("s_win")
        s_acc = sem("s_acc")
        s_far_hot = sem("s_far_hot")
        s_far_win = sem("s_far_win")
        s_agg = sem("s_agg")
        s_aggc = sem("s_aggc")
        s_wsum = sem("s_wsum")
        s_upre = sem("s_upre")
        s_ugelu = sem("s_ugelu")
        s_upd = sem("s_upd")
        s_updr = sem("s_updr")
        s_var = sem("s_var")
        s_rstd = sem("s_rstd")
        s_xs = sem("s_xs")
        s_xst = sem("s_xst")
        s_xstc = sem("s_xstc")
        s_xsw = [sem(f"s_xsw{u}") for u in range(2)]
        s_idx2 = [sem(f"s_idx2{u}") for u in range(2)]
        s_rows2 = [sem(f"s_rows2{u}") for u in range(2)]
        s_hot2 = sem("s_hot2")
        s_win2 = [sem(f"s_win2{u}") for u in range(2)]
        s_acc2 = sem("s_acc2")
        s_far_hot2 = sem("s_far_hot2")
        s_far_win2 = sem("s_far_win2")
        s_a2c = sem("s_a2c")
        s_fin = sem("s_fin")
        s_finr = sem("s_finr")
        s_var2 = sem("s_var2")
        s_rstd2 = sem("s_rstd2")
        s_y = sem("s_y")
        s_out = [sem(f"s_out{u}") for u in range(2)]

        def at(eng, place):
            return place if isinstance(place, int) else eng.snap(place)

        def turns(eng, count, turn):
            turn(0, True, False)
            with eng.Fori(1, count - 1) as i:
                turn(i, False, False)
            turn(count - 1, False, True)

        edge_view = t["edge_t"].rearrange("p (g c) -> p g c", g=NG)
        src_view = t["src_t"].rearrange("p (g c) -> p g c", g=NG)
        xt_view = t["x_t"]
        tab_view = hidden_table.rearrange("(r b p) c -> p r b c", p=P, b=BR)
        x1s_view = x1s_table.rearrange("(r b p) c -> p r b c", p=P, b=BR)
        out_view = out.rearrange("(r b p) c -> p r b c", p=P, b=BR)
        hn_flat = [h[:, :, :].rearrange("p b c -> p (b c)") for h in hn]

        WTS = [(w1x[0:ND, 0:ND], t["mW1"][0:ND, :]), (w1x[0:ND, ND:HC], t["gW1"][0:ND, :]),
               (w1x[ND:ND + 1, 0:ND], t["mb1"]), (w1x[ND:ND + 1, ND:HC], t["gb1"])]
        for j in range(4):
            WTS.append((w1e[ED * j:ED * (j + 1), 0:ND], t["mW1"][ND:ND + ED, :]))
            WTS.append((w1e[ED * j:ED * (j + 1), ND:HC], t["gW1"][ND:ND + ED, :]))
        WTS += [(gw2[:, :], t["gW2"]), (gb2[:, :], t["gb2"]),
                (mw2[0:ND, :], t["mW2"]), (mw2[ND:ND + 1, :], t["mb2"]),
                (uw1x[0:ND, :], t["uW1"][0:ND, :]), (uw1x[ND:ND + 1, :], t["ub1"]),
                (uw1a[:, :], t["uW1"][ND:HC, :]),
                (uw2[0:ND, :], t["uW2"]), (uw2[ND:ND + 1, :], t["ub2"]),
                (w_gcn[:, :], t["W"]), (ln_g[:, :], t["ln_g"]), (ln_b[:, :], t["ln_b"]),
                (b_gcn[:, :], t["b"]),
                (x_t[0:ND, :], t["x_t"]), (x_nat[:, :, :], t["x_nat"].rearrange("(b p) c -> p b c", p=P))]
        WTS_LANDED = 16 * len(WTS)

        block = ctx.enter_context(nc.Block())

        @block.sync
        def _(sp):
            sp.dma_start(dst_rows[:, :], t["dst_rows"]).then_inc(s_dst, 16)
            sp.dma_start(dst_i[:, :], t["dst_t"]).then_inc(s_dst, 16)
            sp.dma_start(weight[:, :], t["weight_t"]).then_inc(s_dst, 16)

            def table_round(i, first, last):
                for u in range(2):
                    node = at(sp, RN * (2 * i + u))
                    if not first:
                        sp.wait_ge(s_tab_mm, 3 * (2 * i + u - 1))
                    sp.dma_start(x_blk[u][0:ND, :], xt_view[:, ds(node, RN)]).then_inc(s_xblk[u], 16)
            for n, (dst, src) in enumerate(WTS):
                if n == 4:
                    table_round(0, True, False)
                sp.dma_start(dst, src).then_inc(s_wts, 16)

            def table_store(r, u):
                r = at(sp, r)
                sp.wait_ge(s_tab_a, 3 * (r + 1))
                sp.dma_start(tab_view[:, ds(r, 1)], rows[u][:, 0:BR, :].rearrange("p (o b) c -> p o b c", o=1)).then_inc(s_tab_w[u], 16)

            def table_turn(i, first, last):
                if not first:
                    table_round(i, False, last)
                for u in range(2):
                    table_store(2 * i + u, u)
            turns(sp, NR // 2, table_turn)

            def load_turn(i, first, last):
                for u in range(2):
                    g = at(sp, 2 * i + u)
                    if not first:
                        sp.wait_ge(s_hid[u], i)
                    sp.dma_start(idx[u][:, :], src_view[:, ds(g, 1), :].rearrange("p o c -> p (o c)")).then_inc(s_idx[u], 16)
                    sp.dma_start(edge_t[u][:, :], edge_view[:, ds(g, 1), :].rearrange("p o c -> p (o c)")).then_inc(s_edge[u], 16)
            turns(sp, TURNS, load_turn)

            def x1s_turn(i, first, last):
                for u in range(2):
                    r = at(sp, 2 * i + u)
                    sp.wait_ge(s_xs, r + 1)
                    sp.dma_start(x1s_view[:, ds(r, 1)], xs[u][:, :, :].rearrange("p (o b) c -> p o b c", o=1)).then_inc(s_xsw[u], 16)
            for u in range(2):
                sp.wait_ge(s_rows[u], 16 * TG * TURNS)

            def idx_turn(i, first, last):
                for u in range(2):
                    g = at(sp, 2 * i + u)
                    if not first:
                        sp.wait_ge(s_win2[u], i)
                    sp.dma_start(idx[u][:, :], src_view[:, ds(g, 1), :].rearrange("p o c -> p (o c)")).then_inc(s_idx2[u], 16)
            turns(sp, NR // 2, x1s_turn)
            turns(sp, TURNS, idx_turn)

            def out_turn(i, first, last):
                for u in range(2):
                    r = at(sp, 2 * i + u)
                    sp.wait_ge(s_y, r + 1)
                    sp.dma_start(out_view[:, ds(r, 1)], xs[u][:, :, :].rearrange("p (o b) c -> p o b c", o=1)).then_inc(s_out[u], 16)
            turns(sp, NR // 2, out_turn)
            for u in range(2):
                sp.wait_ge(s_out[u], 16 * (NR // 2))

        @block.gpsimd
        def _(pool):
            n_const = 0

            def const(ins):
                ins.then_inc(s_const, 1)
                return 1
            n_const += const(nc.gpsimd.memset(ident[:, :], 0.0))
            n_const += const(nc.gpsimd.memset(ones[:, :], 1.0))
            n_const += const(nc.gpsimd.memset(minus_half[:, :], -0.5))
            n_const += const(nc.gpsimd.iota(iota_i[:, :], [[1, W]], base=0, channel_multiplier=0))
            n_const += const(nc.gpsimd.iota(win_i[:, :], [[W, NW]], base=0, channel_multiplier=0))
            pool.wait_ge(s_const, n_const)
            n_const += const(nc.gpsimd.affine_select(out=ident[:, :], in_=ident[:, :], compare_op=ALU.not_equal, fill=1.0,
                                                     base=0, pattern=[[-1, P]], channel_multiplier=1))
            n_const += const(nc.gpsimd.affine_select(out=before[:, :], in_=ones[:, 0:NG], compare_op=ALU.is_gt, fill=0.0,
                                                     base=0, pattern=[[1, NG]], channel_multiplier=-1))
            n_const += const(nc.gpsimd.affine_select(out=pick_w[:, :], in_=ones[:, 0:1], compare_op=ALU.is_gt, fill=0.0,
                                                     base=-ND, pattern=[[0, 1]], channel_multiplier=1))
            assert n_const == N_CONST

            for u in range(2):
                pool.wait_ge(s_tab_w[u], 16 * (NR // 2))

            def gather_turn(landed):
                for u in range(2):
                    pool.wait_ge(s_tab_w[u], 16 * (NR // 2))
                    pool.wait_ge(s_idx[u], landed)
                    for k in range(TG):
                        nc.gpsimd.indirect_dma_start(
                            out=rows[u][:, k, :], out_offset=None, in_=hidden_table,
                            in_offset=bass.IndirectOffsetOnAxis(ap=idx[u][:, k:k + 1], axis=0)).then_inc(s_rows[u], 16)
            with pool.Fori(16, 16 * TURNS + 1, 16) as landed:
                gather_turn(landed)

            def root_turn(i, first, last):
                for u in range(2):
                    for k in range(2):
                        pool.wait_ge(s_var, 2 * (2 * i + u) + k + 1)
                        last_ins = nc.gpsimd.tensor_tensor(rstd[:, :], vare[:, :], minus_half[:, :], ALU.pow)
                        if k == 0:
                            last_ins = nc.gpsimd.tensor_tensor(degp[:, :], degm[:, :], minus_half[:, :], ALU.pow)
                        last_ins.then_inc(s_rstd, 1)
            turns(pool, NR // 2, root_turn)

            for u in range(2):
                pool.wait_ge(s_xsw[u], 16 * (NR // 2))

            def gather2_turn(landed):
                for u in range(2):
                    pool.wait_ge(s_xsw[u], 16 * (NR // 2))
                    pool.wait_ge(s_idx2[u], landed)
                    for k in range(TG):
                        nc.gpsimd.indirect_dma_start(
                            out=hid[u][:, k, 0:ND], out_offset=None, in_=x1s_table,
                            in_offset=bass.IndirectOffsetOnAxis(ap=idx[u][:, k:k + 1], axis=0)).then_inc(s_rows2[u], 16)
            with pool.Fori(16, 16 * TURNS + 1, 16) as landed:
                gather2_turn(landed)

            def root2_turn(i, first, last):
                for u in range(2):
                    pool.wait_ge(s_var2, 2 * i + u + 1)
                    nc.gpsimd.tensor_tensor(rstd[:, :], vare[:, :], minus_half[:, :], ALU.pow).then_inc(s_rstd2, 1)
            turns(pool, NR // 2, root2_turn)

        @block.tensor
        def _(pe):
            pe.wait_ge(s_const, N_CONST)
            pe.wait_ge(s_spread, 1)
            nc.tensor.matmul(bank[7][:, 0:3 * NG], ones[0:NG, :], spread[:, :, :].rearrange("p a g -> p (a g)"),
                             start=True, stop=True).then_inc(s_bcast, 1)

            pe.wait_ge(s_wts, WTS_LANDED)
            pe.wait_ge(s_zero, 1)

            def table_turn(i, first, last):
                for u in range(2):
                    pe.wait_ge(s_xblk[u], 16 * (i + 1))
                    for k in range(BR):
                        m = k // 2
                        if k % 2 == 0 and not first:
                            pe.wait_ge(s_tab_a, 3 * (2 * i + u - 2) + m + 1)
                        mm = nc.tensor.matmul(bank[3 * u + m][:, HC * (k % 2):HC * (k % 2 + 1)],
                                              x_blk[u][:, P * k:P * (k + 1)], w1x[:, :], start=True, stop=True)
                        if k % 2 == 1 or k == BR - 1:
                            mm.then_inc(s_tab_mm, 1)
            turns(pe, NR // 2, table_turn)
            pe.wait_ge(s_tab_a, 3 * NR)
            pe.wait_ge(s_steer, 1)

            def hidden_products(g, u, i, first):
                pe.wait_ge(s_edge[u], 16 * (i + 1))
                for q in range(2):
                    for j in range(4):
                        if q == 0 and not first:
                            pe.wait_ge(s_sum, 4 * (g - 1) + j + 1)
                        mm = nc.tensor.matmul(bank[j][:, HC * q:HC * (q + 1)],
                                              edge_t[u][ED * j:ED * (j + 1), P * q:P * (q + 1)],
                                              w1e[ED * j:ED * (j + 1), :], start=True, stop=True)
                        if q == 1:
                            mm.then_inc(s_pre, 1)

            def window_products(g, u, first):
                pe.wait_ge(s_vals, g + 1)
                for k in range(TG):
                    mm = nc.tensor.matmul(bank[4 + u][0:VC, 0:W], vals[u][:, k, :], hot[u][:, k, :],
                                          start=(k == 0), stop=(k == TG - 1))
                mm.then_inc(s_win, 1)
                more = pe.value_load(steer[0:1, 1, ds(g, 1)], min_val=0, max_val=NW - 1)
                with pe.If(more > 0):
                    done = pe.value_load(steer[0:1, 2, ds(g, 1)], min_val=0, max_val=NW * NG)
                    with pe.Fori(1, more + 1) as w:
                        pe.wait_ge(s_far_hot, done + w)
                        for k in range(TG):
                            mm = nc.tensor.matmul(bank[6][0:VC, 0:W], vals[u][:, k, :], far_hot[:, k, :],
                                                  start=(k == 0), stop=(k == TG - 1))
                        mm.then_inc(s_far_win, 1)

            hidden_products(0, 0, 0, True)

            def pass1_turn(i, first, last):
                hidden_products(2 * i + 1, 1, i, False)
                if not first:
                    pe.wait_ge(s_acc, 2 * i - 1)
                window_products(2 * i, 0, first)
                if not last:
                    hidden_products(2 * i + 2, 0, i + 1, False)
                if not first:
                    pe.wait_ge(s_acc, 2 * i)
                window_products(2 * i + 1, 1, first)
            turns(pe, TURNS, pass1_turn)

            pe.wait_ge(s_acc, NG)

            def node_turn(i, first, last):
                for u in range(2):
                    r = 2 * i + u
                    if not (first and u == 0):
                        pe.wait_ge(s_aggc, 2 * r)
                    for h in range(2):
                        nc.tensor.matmul(bank[h][0:ND, 0:RH], mw2[:, :], acc1[0:ND + 1, ds(RN * r + RH * h, RH)],
                                         start=True, stop=True).then_inc(s_agg, 1)
                    if not (first and u == 0):
                        pe.wait_ge(s_ugelu, 2 * r)
                    for h in range(2):
                        nc.tensor.matmul(bank[2 + h][0:ND, 0:RH], uw1x[:, :], x_t[:, ds(RN * r + RH * h, RH)],
                                         start=True, stop=False)
                        pe.wait_ge(s_aggc, 2 * r + h + 1)
                        nc.tensor.matmul(bank[2 + h][0:ND, 0:RH], uw1a[:, :], agg_t[u][:, RH * h:RH * (h + 1)],
                                         start=False, stop=True).then_inc(s_upre, 1)
                    pe.wait_ge(s_ugelu, 2 * r + 2)
                    pe.wait_ge(s_wsum, r + 1)
                    if not (first and u == 0):
                        pe.wait_ge(s_updr, r)
                    for k in range(BR):
                        nc.tensor.matmul(bank[5][:, k:k + 1], wsum[u][ND:VC, P * k:P * (k + 1)], pick_w[ND:VC, :],
                                         start=True, stop=True)
                    for k in range(BR):
                        mm = nc.tensor.matmul(bank[4][:, ND * k:ND * (k + 1)], upd_t[u][:, P * k:P * (k + 1)], uw2[:, :],
                                              start=True, stop=True)
                    mm.then_inc(s_upd, 1)
                    pe.wait_ge(s_xs, r + 1)
                    if not (first and u == 0):
                        pe.wait_ge(s_xstc, 2 * r)
                    for k in range(BR):
                        mm = nc.tensor.transpose(bank[6 + k // 3][0:ND, P * (k % 3):P * (k % 3 + 1)], xs[u][:, k, :], ident[:, :])
                        if k == 2 or k == BR - 1:
                            mm.then_inc(s_xst, 1)
            turns(pe, NR // 2, node_turn)

            pe.wait_ge(s_xstc, 2 * NR)

            def window2_products(g, u, i, first):
                pe.wait_ge(s_rows2[u], 16 * TG * (i + 1))
                pe.wait_ge(s_hot2, g + 1)
                if not first:
                    pe.wait_ge(s_acc2, g - 1)
                for k in range(TG):
                    mm = nc.tensor.matmul(bank[4 + u][0:ND, 0:W], hid[u][:, k, 0:ND], hot[u][:, k, :],
                                          start=(k == 0), stop=(k == TG - 1))
                more = pe.value_load(steer[0:1, 1, ds(g, 1)], min_val=0, max_val=NW - 1)
                mm.then_inc(s_win2[u], 1)
                with pe.If(more > 0):
                    done = pe.value_load(steer[0:1, 2, ds(g, 1)], min_val=0, max_val=NW * NG)
                    with pe.Fori(1, more + 1) as w:
                        pe.wait_ge(s_far_hot2, done + w)
                        for k in range(TG):
                            mm = nc.tensor.matmul(bank[6][0:ND, 0:W], hid[u][:, k, 0:ND], far_hot[:, k, :],
                                                  start=(k == 0), stop=(k == TG - 1))
                        mm.then_inc(s_far_win2, 1)

            def pass2_turn(i, first, last):
                for u in range(2):
                    window2_products(2 * i + u, u, i, first)
            turns(pe, TURNS, pass2_turn)

            def final_turn(i, first, last):
                for u in range(2):
                    r = 2 * i + u
                    pe.wait_ge(s_a2c, r + 1)
                    if not first:
                        pe.wait_ge(s_finr, r - 1)
                    for k in range(BR):
                        mm = nc.tensor.matmul(bank[u][:, ND * k:ND * (k + 1)], agg_t[u][:, P * k:P * (k + 1)], w_gcn[:, :],
                                              start=True, stop=True)
                    mm.then_inc(s_fin, 1)
            turns(pe, NR // 2, final_turn)

        @block.scalar
        def _(act):
            def table_turn(i, first, last):
                for u in range(2):
                    r = 2 * i + u
                    if not first:
                        act.wait_ge(s_tab_w[u], 16 * i)
                    for m in range(3):
                        cols = HC * min(2, BR - 2 * m)
                        act.wait_ge(s_tab_mm, 3 * r + m + 1)
                        nc.scalar.activation(rows[u][:, 2 * m:min(2 * m + 2, BR), :].rearrange("p b c -> p (b c)"),
                                             bank[3 * u + m][:, 0:cols], ACT.Copy).then_inc(s_tab_a, 1)
            turns(act, NR // 2, table_turn)
            act.wait_ge(s_zero, 1)

            def pass1_turn(i, first, last):
                for u in range(2):
                    g = 2 * i + u
                    if not first:
                        act.wait_ge(s_vals, g - 1)
                    for j in range(4):
                        act.wait_ge(s_sum, 4 * g + j + 1)
                        gelu = nc.scalar.activation(hid[u][:, 2 * j:2 * j + 2, :].rearrange("p b c -> p (b c)"),
                                                    rows[u][:, 2 * j:2 * j + 2, :].rearrange("p b c -> p (b c)"),
                                                    ACT.Gelu)
                    gelu.then_inc(s_hid[u], 1)
                    act.wait_ge(s_logit, g + 1)
                    nc.scalar.activation(squash[u][:, :], logit[u][:, :], ACT.Tanh, bias=half_gb2[:, :],
                                         scale=0.5).then_inc(s_squash, 1)
            turns(act, TURNS, pass1_turn)

            act.wait_ge(s_acc, NG)

            def node_turn(i, first, last):
                for u in range(2):
                    r = 2 * i + u
                    if not first:
                        act.wait_ge(s_upd, r - 1)
                    nc.scalar.activation(wsum[u][ND:VC, :], acc1[ND:VC, ds(RN * r, RN)], ACT.Copy).then_inc(s_wsum, 1)
                    for h in range(2):
                        act.wait_ge(s_agg, 2 * r + h + 1)
                        nc.scalar.activation(agg_t[u][:, RH * h:RH * (h + 1)], bank[h][0:ND, 0:RH],
                                             ACT.Copy).then_inc(s_aggc, 1)
                    for h in range(2):
                        act.wait_ge(s_upre, 2 * r + h + 1)
                        nc.scalar.activation(upd_t[u][0:ND, RH * h:RH * (h + 1)], bank[2 + h][0:ND, 0:RH],
                                             ACT.Gelu).then_inc(s_ugelu, 1)
                    for h in range(2):
                        cols = P * min(3, BR - 3 * h)
                        act.wait_ge(s_xst, 2 * r + h + 1)
                        nc.scalar.activation(acc2[:, ds(RN * r + 3 * P * h, cols)], bank[6 + h][0:ND, 0:cols],
                                             ACT.Copy).then_inc(s_xstc, 1)
            turns(act, NR // 2, node_turn)

            act.wait_ge(s_acc2, NG)

            def final_turn(i, first, last):
                for u in range(2):
                    if not first:
                        act.wait_ge(s_fin, 2 * i + u - 1)
                    nc.scalar.activation(agg_t[u][:, :], acc2[:, ds(RN * (2 * i + u), RN)], ACT.Copy).then_inc(s_a2c, 1)
            turns(act, NR // 2, final_turn)

        @block.vector
        def _(dve):
            nc.vector.memset(acc1[:, :], 0.0)
            nc.vector.memset(acc2[:, NP:AW], 0.0)
            for u in range(2):
                nc.vector.memset(x_blk[u][ND:ND + 1, :], 1.0)
                nc.vector.memset(upd_t[u][ND:ND + 1, :], 1.0)
            nc.vector.memset(x_t[ND:ND + 1, :], 1.0).then_inc(s_zero, 1)

            chain = [0]

            def link(ins):
                chain[0] += 1
                ins.then_inc(s_chain, 1)
                dve.wait_ge(s_chain, chain[0])

            dve.wait_ge(s_const, N_CONST)
            dve.wait_ge(s_dst, 48)
            nc.vector.tensor_copy(iota_w[:, :], iota_i[:, :])
            nc.vector.tensor_copy(win_off[:, :], win_i[:, :])
            nc.vector.tensor_reduce(lo[:, :], dst_rows[:, :], AX, ALU.min)
            link(nc.vector.tensor_reduce(hi[:, :], dst_rows[:, :], AX, ALU.max))
            link(nc.vector.tensor_tensor(reach[:, :], hi[:, :], lo[:, :], ALU.subtract))
            link(nc.vector.tensor_scalar(crossed[:, 1:NW], win_off[0:NG, 1:NW], reach[:, :], None, ALU.is_le))
            link(nc.vector.tensor_reduce(extra[:, :], crossed[:, 1:NW], AX, ALU.add))
            nc.vector.tensor_scalar(spread[:, 0, :], ident[0:NG, 0:NG], lo[:, :], None, ALU.mult)
            nc.vector.tensor_scalar(spread[:, 1, :], ident[0:NG, 0:NG], extra[:, :], None, ALU.mult)
            nc.vector.tensor_scalar(spread[:, 2, :], before[0:NG, :], extra[:, :], None, ALU.mult).then_inc(s_spread, 1)
            dve.wait_ge(s_bcast, 1)
            nc.vector.tensor_copy(steer[0:1, :, :].rearrange("p a g -> p (a g)"), bank[7][0:1, 0:3 * NG])
            link(nc.vector.tensor_copy(lo_all[:, :], bank[7][:, 0:NG]))
            dve.wait_ge(s_wts, WTS_LANDED)
            nc.vector.tensor_scalar(half_gb2[:, :], gb2[:, :], 0.5, None, ALU.mult).then_inc(s_steer, 1)
            link(nc.vector.tensor_tensor(dst_rel[:, :].rearrange("p (g k) -> p g k", k=TG),
                                         dst_i[:, :].rearrange("p (g k) -> p g k", k=TG),
                                         lo_all[:, :].rearrange("p (g o) -> p g o", o=1).to_broadcast([P, NG, TG]),
                                         ALU.subtract))
            SETUP = chain[0]

            def one_hot(place, rel):
                return nc.vector.tensor_tensor(
                    place[:, :, :], rel.rearrange("p (k o) -> p k o", o=1).to_broadcast([P, TG, W]),
                    iota_w[:, :].rearrange("p (o w) -> p o w", o=1).to_broadcast([P, TG, W]), ALU.is_equal)

            def take_window(acc, rws, g, u, win_sem, win_count, acc_sem, far_hot_sem, far_win_sem, weigh):
                nc.vector.drain()
                dve.wait_ge(win_sem, win_count)
                first_node = dve.value_load(steer[0:1, 0, ds(g, 1)], min_val=0, max_val=NP - 1)
                nc.vector.tensor_tensor(acc[0:rws, ds(first_node, W)], acc[0:rws, ds(first_node, W)],
                                        bank[4 + u][0:rws, 0:W], ALU.add).then_inc(acc_sem, 1)
                more = dve.value_load(steer[0:1, 1, ds(g, 1)], min_val=0, max_val=NW - 1)
                with dve.If(more > 0):
                    done = dve.value_load(steer[0:1, 2, ds(g, 1)], min_val=0, max_val=NW * NG)
                    with dve.Fori(1, more + 1) as w:
                        nc.vector.tensor_scalar(far_rel[:, :], dst_rel[:, ds(TG * g, TG)], win_off[:, ds(w, 1)], None,
                                                ALU.subtract)
                        nc.vector.drain()
                        if weigh:
                            one_hot(far_hot, far_rel[:, :])
                            nc.vector.drain()
                            weigh_hot(far_hot, g).then_inc(far_hot_sem, 1)
                        else:
                            one_hot(far_hot, far_rel[:, :]).then_inc(far_hot_sem, 1)
                        dve.wait_ge(far_win_sem, done + w)
                        at = nc.s_assert_within(dve.snap(first_node + w * W), 0, AW - W)
                        nc.vector.tensor_tensor(acc[0:rws, ds(at, W)], acc[0:rws, ds(at, W)],
                                                bank[6][0:rws, 0:W], ALU.add)
                        nc.vector.drain()

            def weigh_hot(place, g):
                return nc.vector.tensor_tensor(
                    place[:, :, :], place[:, :, :],
                    weight[:, ds(TG * g, TG)].rearrange("p (k o) -> p k o", o=1).to_broadcast([P, TG, W]), ALU.mult)

            def pass1_turn(i, first, last):
                for u in range(2):
                    g = 2 * i + u
                    dve.wait_ge(s_rows[u], 16 * TG * (i + 1))
                    for j in range(4):
                        dve.wait_ge(s_pre, 4 * g + j + 1)
                        pair = rows[u][:, 2 * j:2 * j + 2, :].rearrange("p b c -> p (b c)")
                        nc.vector.tensor_tensor(pair, pair, bank[j][:, 0:2 * HC], ALU.add).then_inc(s_sum, 1)
                    if not first:
                        dve.wait_ge(s_win, g - 1)
                    one_hot(hot[u], dst_rel[:, ds(TG * g, TG)])
                    nc.vector.tensor_copy(vals[u][:, :, ND + 1:VC],
                                          weight[:, ds(TG * g, TG)].rearrange("p (k o) -> p k o", o=1))
                    if not (first and u == 0):
                        take_window(acc1, VC, g - 1, 1 - u, s_win, g, s_acc, s_far_hot, s_far_win, False)
                    dve.wait_ge(s_hid[u], i + 1)
                    nc.vector.tensor_tensor(prod[:, :, :], hid[u][:, :, ND:HC],
                                            gw2[:, :].rearrange("p (o c) -> p o c", o=1).to_broadcast([P, TG, ND]), ALU.mult)
                    nc.vector.drain()
                    nc.vector.tensor_reduce(logit[u][:, :], prod[:, :, :], AX, ALU.add).then_inc(s_logit, 1)
                    dve.wait_ge(s_squash, g + 1)
                    nc.vector.tensor_scalar(vals[u][:, :, ND:ND + 1], squash[u][:, :].rearrange("p (k o) -> p k o", o=1),
                                            0.5, 0.5, ALU.mult, ALU.add)
                    nc.vector.drain()
                    nc.vector.tensor_tensor(vals[u][:, :, 0:ND], hid[u][:, :, 0:ND],
                                            vals[u][:, :, ND:ND + 1].to_broadcast([P, TG, ND]), ALU.mult).then_inc(s_vals, 1)
            turns(dve, TURNS, pass1_turn)
            take_window(acc1, VC, NG - 1, 1, s_win, NG, s_acc, s_far_hot, s_far_win, False)

            def norm(src, dst, ready, done, count):
                for k in range(BR):
                    nc.vector.bn_stats(stats[:, k, :], src[:, k, :])
                nc.vector.drain()
                for k in range(BR):
                    nc.vector.bn_aggr(mv[:, k, :], stats[:, k, :])
                nc.vector.drain()
                nc.vector.tensor_scalar(vare[:, :].rearrange("p (b o) -> p b o", o=1), mv[:, :, 1:2], EPS, None,
                                        ALU.add).then_inc(ready, 1)
                dve.wait_ge(done, count)
                for k in range(BR):
                    nc.vector.tensor_scalar(dst[:, k, :], src[:, k, :], mv[:, k, 0:1], rstd[:, k:k + 1],
                                            ALU.subtract, ALU.mult)
                nc.vector.drain()

            def node_turn(i, first, last):
                for u in range(2):
                    r = 2 * i + u
                    blocks = ds(BR * r, BR)
                    h = hn[u]
                    dve.wait_ge(s_upd, r + 1)
                    nc.vector.tensor_tensor(h[:, :, :], x_nat[:, blocks, :], bank[4][:, 0:BR * ND].rearrange("p (b c) -> p b c", b=BR),
                                            ALU.add)
                    nc.vector.tensor_scalar(degs[:, :], bank[5][:, 0:BR], 1.0, None, ALU.add).then_inc(s_updr, 1)
                    nc.vector.drain()
                    nc.vector.tensor_scalar(degm[:, :], degs[:, :], 1e-30, None, ALU.max)
                    norm(h, h, s_var, s_rstd, 2 * r + 1)
                    nc.vector.tensor_scalar(degs[:, :], degs[:, :], 0.0, None, ALU.is_gt)
                    nc.vector.tensor_tensor(h[:, :, :], h[:, :, :], ln_g[:, :].rearrange("p (o c) -> p o c", o=1).to_broadcast([P, BR, ND]), ALU.mult)
                    nc.vector.drain()
                    nc.vector.tensor_tensor(dinv[:, blocks], degp[:, :], degs[:, :], ALU.mult)
                    nc.vector.tensor_tensor(h[:, :, :], h[:, :, :], ln_b[:, :].rearrange("p (o c) -> p o c", o=1).to_broadcast([P, BR, ND]), ALU.add)
                    nc.vector.drain()
                    nc.vector.tensor_tensor(h[:, :, :], h[:, :, :], x_nat[:, blocks, :], ALU.add)
                    nc.vector.drain()
                    norm(h, h, s_var, s_rstd, 2 * r + 2)
                    if not first:
                        dve.wait_ge(s_xsw[u], 16 * i)
                        dve.wait_ge(s_xst, 2 * (r - 1))
                    nc.vector.tensor_tensor(xs[u][:, :, :], h[:, :, :],
                                            dinv[:, blocks].rearrange("p (b o) -> p b o", o=1).to_broadcast([P, BR, ND]),
                                            ALU.mult).then_inc(s_xs, 1)
                    nc.vector.tensor_tensor(x1[:, blocks, :], h[:, :, :],
                                            b_gcn[:, :].rearrange("p (o c) -> p o c", o=1).to_broadcast([P, BR, ND]), ALU.add)
            turns(dve, NR // 2, node_turn)
            dve.wait_ge(s_xstc, 2 * NR)

            def pass2_turn(i, first, last):
                for u in range(2):
                    g = 2 * i + u
                    if not first:
                        dve.wait_ge(s_win2[u], i)
                    one_hot(hot[u], dst_rel[:, ds(TG * g, TG)])
                    nc.vector.drain()
                    weigh_hot(hot[u], g).then_inc(s_hot2, 1)
                    if not (first and u == 0):
                        take_window(acc2, ND, g - 1, 1 - u, s_win2[1 - u], i + u, s_acc2, s_far_hot2, s_far_win2, True)
            turns(dve, TURNS, pass2_turn)
            take_window(acc2, ND, NG - 1, 1, s_win2[1], TURNS, s_acc2, s_far_hot2, s_far_win2, True)

            def final_turn(i, first, last):
                for u in range(2):
                    r = 2 * i + u
                    h = hn[u]
                    dve.wait_ge(s_fin, r + 1)
                    for k in range(BR):
                        mv_ = nc.vector.tensor_scalar(h[:, k, :], bank[u][:, ND * k:ND * (k + 1)],
                                                      dinv[:, ds(BR * r + k, 1)], None, ALU.mult)
                    mv_.then_inc(s_finr, 1)
                    nc.vector.drain()
                    nc.vector.tensor_tensor(h[:, :, :], h[:, :, :], x1[:, ds(BR * r, BR), :], ALU.add)
                    nc.vector.drain()
                    if not first:
                        dve.wait_ge(s_out[u], 16 * i)
                    norm(h, xs[u], s_var2, s_rstd2, r + 1)
                    nc.vector.tensor_copy(stats[:, 0, 0:1], vare[:, 0:1]).then_inc(s_y, 1)
            turns(dve, NR // 2, final_turn)


N_CONST = 8


def kernel(**inputs):
    import numpy as np
    import concourse.bacc as bacc
    from concourse import mybir as mb
    from concourse.bass_utils import run_bass_kernel_spmd

    a = {k.replace("L0_gnn_", "").replace("L1_gnn_", ""): np.asarray(v) for k, v in inputs.items()}
    EPAD = NT * P

    def by_tile(v, fill):
        full = np.full((EPAD,), fill, v.dtype)
        full[:E] = v
        return full.reshape(NT, P).T

    x = np.zeros((NP, ND), np.float32)
    x[:N] = a["x"]
    edge = np.zeros((EPAD, ED), np.float32)
    edge[:E] = a["edge_attr_32"]
    dst = np.full((EPAD,), N, np.int32)
    dst[:E] = a["dst"]
    rep = lambda v: np.broadcast_to(v.reshape(1, -1), (P, v.size))
    arrays = {
        "x_t": x.T,
        "x_nat": x,
        "src_t": by_tile(a["src"].astype(np.int32), 0),
        "dst_t": by_tile(a["dst"].astype(np.int32), N),
        "dst_rows": dst.reshape(NG, GE),
        "weight_t": by_tile(a["edge_weight"], 0),
        "edge_t": edge.reshape(NG, 4, 2, P, ED).transpose(1, 4, 0, 2, 3).reshape(P, NG * 2 * P),
        "mW1": a["mW1"], "gW1": a["gW1"], "mb1": a["mb1"].reshape(1, ND), "gb1": a["gb1"].reshape(1, ND),
        "gW2": rep(a["gW2"]), "gb2": rep(a["gb2"]),
        "mW2": a["mW2"], "mb2": a["mb2"].reshape(1, ND),
        "uW1": a["uW1"], "ub1": a["ub1"].reshape(1, ND), "uW2": a["uW2"], "ub2": a["ub2"].reshape(1, ND),
        "W": a["W"], "ln_g": rep(a["ln_g"]), "ln_b": rep(a["ln_b"]), "b": rep(a["b"]),
    }
    arrays = {f"in_{k}": np.ascontiguousarray(v) for k, v in arrays.items()}
    nc = bacc.Bacc("TRN2", target_bir_lowering=False, num_devices=1)
    t = {k[3:]: nc.dram_tensor(k, v.shape, mb.dt.from_np(v.dtype), kind="ExternalInput").ap() for k, v in arrays.items()}
    out = nc.dram_tensor("out_nodes", (NP, ND), mb.dt.float32, kind="ExternalOutput").ap()
    gnn_kernel(nc, t, out)
    r = run_bass_kernel_spmd(nc, [arrays], core_ids=[0])
    return r.results[0]["out_nodes"][:N]
```

```python
import concourse.bass as bass
from concourse import mybir
from contextlib import ExitStack

P = 128
N, E = 6250, 100000
ND, ED = 96, 32
TG = 8
GE = TG * P
TURNS = -(-E // (2 * GE))
NG = 2 * TURNS
NT = NG * TG
NB = -(-N // P)
NP = NB * P
W = 80
NW = -(-NP // W)
AW = NP + 2 * W
VC = ND + 2
HC = 2 * ND
SLOTS = 4
PAIRS = TURNS // 2
PEELED = 3
LAG = 2
SQUASH_AFTER = (0, 3)
EPS = 1e-5
ROOT_SEED = float(0x5F3759DF)
assert ND + ED == P and NB == TURNS == 2 * PAIRS + 1


def gnn_kernel(nc, t, out):
    fp32, i32, bf16 = mybir.dt.float32, mybir.dt.int32, mybir.dt.bfloat16
    ALU = mybir.AluOpType
    ACT = mybir.ActivationFunctionType
    AX = mybir.AxisListType.X
    ds = bass.ds

    x1s_table = nc.dram_tensor("x1s_table", [NP, ND], fp32, kind="Internal").ap()

    ctx = ExitStack()
    with ctx:
        def sb(name, shape, dt=fp32):
            return ctx.enter_context(nc.sbuf_tensor(name, shape, dt))

        def sem(name):
            return ctx.enter_context(nc.semaphore(name))

        ident = sb("ident", [P, P])
        before = sb("before", [P, NG])
        ones = sb("ones", [P, P])
        ones_b = sb("ones_b", [P, P], bf16)
        iota_w = sb("iota_w", [P, W])
        iota_i = sb("iota_i", [P, W], i32)
        win_i = sb("win_i", [P, NW], i32)
        win_off = sb("win_off", [P, NW])
        due_i = sb("due_i", [P, 1], i32)
        due = sb("due", [P, 1])
        pick_w = sb("pick_w", [P, 1])
        w1 = sb("w1", [P, HC])
        b1 = sb("b1", [3, 2, HC])
        b1_rest = sb("b1_rest", [3, 2, HC])
        b1_part = sb("b1_part", [3, 2, HC])
        b1_sum = sb("b1_sum", [3, 2, HC])
        b1_hi = sb("b1_hi", [3, 2, HC], bf16)
        b1_split = sb("b1_split", [P, 2, HC], bf16)
        gw2 = sb("gw2", [P, ND])
        gb2 = sb("gb2", [P, 1])
        half_gb2 = sb("half_gb2", [P, 1])
        mw2 = sb("mw2", [ND + 1, ND])
        uw1x = sb("uw1x", [ND + 1, ND])
        uw1a = sb("uw1a", [ND, ND])
        uw2 = sb("uw2", [ND + 1, ND])
        w_gcn = sb("w_gcn", [ND, ND])
        ln_g = sb("ln_g", [P, ND])
        ln_b = sb("ln_b", [P, ND])
        b_gcn = sb("b_gcn", [P, ND])
        dst_rows = sb("dst_rows", [NG, GE], i32)
        lo = sb("lo", [NG, 1])
        hi = sb("hi", [NG, 1])
        reach = sb("reach", [NG, 1])
        crossed = sb("crossed", [NG, NW])
        extra = sb("extra", [NG, 1])
        spread = sb("spread", [NG, 3 * NG + 1])
        lo_all = sb("lo_all", [P, NG])
        steer = sb("steer", [1, 3 * NG + 1], i32)
        dst_i = sb("dst_i", [P, NT], i32)
        dst_rel = sb("dst_rel", [P, NT])
        weight = sb("weight", [P, NT])
        x_t = sb("x_t", [ND + 1, NP])
        x_nat = sb("x_nat", [P, NB, ND])
        x1b = sb("x1b", [P, NB, ND])
        dinv = sb("dinv", [P, NB])
        acc1 = sb("acc1", [VC, AW])
        acc2 = sb("acc2", [ND, AW])
        idx = [sb(f"idx{v}", [P, TG], i32) for v in range(SLOTS)]
        rows = [sb(f"rows{v}", [P, TG, ND]) for v in range(SLOTS)]
        feat = [sb(f"feat{u}", [P, GE]) for u in range(2)]
        hid = [sb(f"hid{u}", [P, TG, HC]) for u in range(2)]
        vals = [sb(f"vals{u}", [P, TG, VC]) for u in range(2)]
        hot = [sb(f"hot{u}", [P, TG, W]) for u in range(2)]
        logit = [sb(f"logit{u}", [P, TG]) for u in range(2)]
        squash = [sb(f"squash{u}", [P, TG]) for u in range(2)]
        prod = sb("prod", [P, TG, ND])
        far_rel = sb("far_rel", [P, TG])
        far_hot = sb("far_hot", [P, TG, W])
        agg_t = sb("agg_t", [ND, P])
        upd_t = sb("upd_t", [ND + 1, P])
        wsum = sb("wsum", [P, P])
        h = sb("h", [P, ND])
        h_g = sb("h_g", [P, ND])
        h2 = sb("h2", [P, ND])
        h2_c = sb("h2_c", [P, ND])
        xs = sb("xs", [P, ND])
        y = sb("y", [P, ND])
        stats = sb("stats", [P, 2, 6])
        mv = sb("mv", [P, 2, 2])
        rin = sb("rin", [P, 3])
        root = sb("root", [P, 3])
        step = sb("step", [P, 3])
        deg = sb("deg", [P, 1])

        def psum(name):
            return ctx.enter_context(nc.psum_tensor(name, [P, 512], fp32))

        ps_xt = [psum(f"ps_xt{k}") for k in range(2)]
        ps_hid = [psum(f"ps_hid{k}") for k in range(2)]
        ps_win = [psum(f"ps_win{k}") for k in range(2)]
        ps_bt = psum("ps_bt")
        ps_bn = psum("ps_bn")

        s_win_in = sem("s_win_in")
        s_dst = sem("s_dst")
        s_w1 = sem("s_w1")
        s_wts = sem("s_wts")
        s_nodes = sem("s_nodes")
        s_const = sem("s_const")
        s_fill = sem("s_fill")
        s_chain = sem("s_chain")
        s_spread = sem("s_spread")
        s_bcast = sem("s_bcast")
        s_steer = sem("s_steer")
        s_bias = sem("s_bias")
        s_idx = [sem(f"s_idx{v}") for v in range(SLOTS)]
        s_edge = [sem(f"s_edge{u}") for u in range(2)]
        s_rows = [sem(f"s_rows{v}") for v in range(SLOTS)]
        s_xt = sem("s_xt")
        s_feat = sem("s_feat")
        s_pre = sem("s_pre")
        s_gelu = sem("s_gelu")
        s_logit = sem("s_logit")
        s_squash = sem("s_squash")
        s_vals = sem("s_vals")
        s_win = sem("s_win")
        s_acc = sem("s_acc")
        s_far_hot = sem("s_far_hot")
        s_far_win = sem("s_far_win")
        s_wsum = sem("s_wsum")
        s_agg = sem("s_agg")
        s_aggc = sem("s_aggc")
        s_upre = sem("s_upre")
        s_ugelu = sem("s_ugelu")
        s_upd = sem("s_upd")
        s_updr = sem("s_updr")
        s_xs = sem("s_xs")
        s_xst = sem("s_xst")
        s_xstc = sem("s_xstc")
        s_xsw = sem("s_xsw")
        s_idx2 = [sem(f"s_idx2{v}") for v in range(SLOTS)]
        s_rows2 = [sem(f"s_rows2{v}") for v in range(SLOTS)]
        s_hot2 = sem("s_hot2")
        s_win2 = [sem(f"s_win2{u}") for u in range(2)]
        s_acc2 = sem("s_acc2")
        s_far_hot2 = sem("s_far_hot2")
        s_far_win2 = sem("s_far_win2")
        s_sum2 = sem("s_sum2")
        s_fin = sem("s_fin")
        s_finr = sem("s_finr")
        s_y = sem("s_y")
        s_out = sem("s_out")

        def at(eng, place):
            return place if isinstance(place, int) else eng.snap(place)

        def wait(eng, s, count):
            if not isinstance(count, int) or count > 0:
                eng.wait_ge(s, count)

        def run_pass(eng, step_fn, block_a=None, block_b=None, even=None, odd=None, ahead=False, close=None, finish=None):
            lag_a = even if odd is None else odd

            def second_part(b):
                if block_b is not None:
                    block_b(b)

            def turn(k, q, easy):
                i = 2 * k + q

                def beside(lag):
                    return None if not easy or lag is None or (isinstance(i, int) and i < lag) else i - lag

                if not (ahead and isinstance(i, int) and i == 0):
                    step_fn(k, 2 * q, easy, beside(even))
                step_fn(k, 2 * q + 1, easy, beside(odd))

            if ahead:
                step_fn(0, 0, True, None)
                eng.wait_ge(s_steer, 1)
            hard = eng.value_load(steer[0:1, 3 * NG:3 * NG + 1], min_val=0, max_val=NG * NW)
            with eng.If(hard < 1):
                for i in range(2 * PEELED):
                    turn(i // 2, i % 2, True)
                with eng.Fori(PEELED, PAIRS) as k:
                    turn(k, 0, True)
                    turn(k, 1, True)
                turn(PAIRS, 0, True)
                if close is not None:
                    close(True)
                if block_b is not None:
                    for b in range(TURNS - even, NB - lag_a - 1):
                        block_b(b)
                if block_a is not None:
                    for b in range(NB - lag_a, NB):
                        block_a(b)
                        second_part(b - 1)
                    second_part(NB - 1)
                if finish is not None:
                    finish()
            with eng.Else():
                turn(0, 0, False)
                turn(0, 1, False)
                with eng.Fori(1, PAIRS) as k:
                    turn(k, 0, False)
                    turn(k, 1, False)
                turn(PAIRS, 0, False)
                if close is not None:
                    close(False)
                if block_a is not None:
                    block_a(0)
                    with eng.Fori(1, NB) as b:
                        block_a(b)
                        second_part(b - 1)
                    second_part(NB - 1)
                if finish is not None:
                    finish()

        def all_added(b):
            return min(2 * b + 3, NG) if isinstance(b, int) else NG

        def spaced(items):
            return items + [None] * (TG // 2 - len(items))

        src_view = t["src_t"].rearrange("p (g c) -> p g c", g=NG)
        edge_view = t["edge_t"].rearrange("f (g c) -> f g c", g=NG)
        x1s_view = x1s_table.rearrange("(b p) c -> p b c", p=P)
        out_view = out.rearrange("(b p) c -> p b c", p=P)

        def flat(ap):
            return ap.rearrange("p a b -> p (a b)")

        WTS = [(w1[:, 0:ND], t["mW1"]), (w1[:, ND:HC], t["gW1"]),
               (b1[:, 0, 0:ND], t["mb1_3"]), (b1[:, 0, ND:HC], t["gb1_3"]),
               (b1[:, 1, 0:ND], t["mb1_3"]), (b1[:, 1, ND:HC], t["gb1_3"]),
               (gw2[:, :], t["gW2"]), (gb2[:, :], t["gb2"]),
               (mw2[0:ND, :], t["mW2"]), (mw2[ND:ND + 1, :], t["mb2"]),
               (uw1x[0:ND, :], t["uW1"][0:ND, :]), (uw1x[ND:ND + 1, :], t["ub1"]),
               (uw1a[:, :], t["uW1"][ND:HC, :]),
               (uw2[0:ND, :], t["uW2"]), (uw2[ND:ND + 1, :], t["ub2"]),
               (w_gcn[:, :], t["W"]), (ln_g[:, :], t["ln_g"]), (ln_b[:, :], t["ln_b"]),
               (b_gcn[:, :], t["b"])]
        N_W1 = 6
        W1_LANDED, WTS_LANDED = 16 * N_W1, 16 * (len(WTS) - N_W1)

        block = ctx.enter_context(nc.Block())

        @block.sync
        def _(sp):
            def load_idx(g, v, sems):
                sp.dma_start(idx[v][:, :], src_view[:, ds(g, 1), :].rearrange("p o c -> p (o c)")).then_inc(sems[v], 16)

            def load1(k, v, easy, b):
                if isinstance(k, int) and k == 0:
                    return
                g = at(sp, SLOTS * k + v)
                sp.wait_ge(s_xt, 2 * g - 6)
                load_idx(g, v, s_idx)

            load_idx(0, 0, s_idx)
            load_idx(1, 1, s_idx)
            sp.dma_start(dst_rows[:, :], t["dst_rows"]).then_inc(s_win_in, 16)
            sp.dma_start(feat[0][ND:P, :], edge_view[:, 0, :]).then_inc(s_edge[0], 16)
            for dst, src in WTS[:N_W1]:
                sp.dma_start(dst, src).then_inc(s_w1, 16)
            load_idx(2, 2, s_idx)
            load_idx(3, 3, s_idx)
            sp.dma_start(dst_i[:, :], t["dst_t"]).then_inc(s_dst, 16)
            sp.dma_start(weight[:, :], t["weight_t"]).then_inc(s_dst, 16)
            for dst, src in WTS[N_W1:]:
                sp.dma_start(dst, src).then_inc(s_wts, 16)
            sp.dma_start(feat[1][ND:P, :], edge_view[:, 1, :]).then_inc(s_edge[1], 16)
            sp.dma_start(x_t[:, :], t["x_t"]).then_inc(s_nodes, 16)
            sp.dma_start(x_nat[:, :, :], t["x_nat"].rearrange("(b p) c -> p b c", p=P)).then_inc(s_nodes, 16)
            run_pass(sp, load1, ahead=True)

            def load2(k, v, easy, b):
                g = at(sp, SLOTS * k + v)
                if isinstance(k, int) and k == 0:
                    sp.wait_ge(s_xt, 2 * (NG - (NG - 1 - v) % SLOTS))
                elif easy:
                    sp.wait_ge(s_win2[v % 2], 2 * k + v // 2 - 1)
                else:
                    sp.wait_ge(s_acc2, g - 3)
                load_idx(g, v, s_idx2)
            run_pass(sp, load2)

        @block.gpsimd
        def _(pool):
            def gathers(landed, v, table, idx_sem, rows_sem, known):
                pool.wait_ge(*known)
                pool.wait_ge(idx_sem[v], landed)
                for k in range(TG):
                    nc.gpsimd.indirect_dma_start(
                        out=rows[v][:, k, :], out_offset=None, in_=table,
                        in_offset=bass.IndirectOffsetOnAxis(ap=idx[v][:, k:k + 1], axis=0)).then_inc(rows_sem[v], 16)

            def const(ins):
                ins.then_inc(s_const, 1)
                return 1
            n_const = 0
            gathers(16, 0, t["x_nat"], s_idx, s_rows, (s_idx[0], 16))
            n_const += const(nc.gpsimd.memset(ident[:, :], 0.0))
            n_const += const(nc.gpsimd.memset(ones[:, :], 1.0))
            n_const += const(nc.gpsimd.memset(ones_b[:, :], 1.0))
            n_const += const(nc.gpsimd.iota(iota_i[:, :], [[1, W]], base=0, channel_multiplier=0))
            n_const += const(nc.gpsimd.iota(win_i[:, :], [[W, NW]], base=0, channel_multiplier=0))
            n_const += const(nc.gpsimd.iota(due_i[:, :], [[0, 1]], base=-P // 2, channel_multiplier=P // 2))
            pool.wait_ge(s_const, n_const)
            n_const += const(nc.gpsimd.affine_select(out=ident[:, :], in_=ident[:, :], compare_op=ALU.not_equal, fill=1.0,
                                                     base=0, pattern=[[-1, P]], channel_multiplier=1))
            n_const += const(nc.gpsimd.affine_select(out=before[:, :], in_=ones[:, 0:NG], compare_op=ALU.is_gt, fill=0.0,
                                                     base=0, pattern=[[1, NG]], channel_multiplier=-1))
            n_const += const(nc.gpsimd.affine_select(out=pick_w[:, :], in_=ones[:, 0:1], compare_op=ALU.is_gt, fill=0.0,
                                                     base=-ND, pattern=[[0, 1]], channel_multiplier=1))
            assert n_const == N_CONST
            for v in range(1, SLOTS):
                gathers(16, v, t["x_nat"], s_idx, s_rows, (s_idx[v], 16))
            with pool.Fori(32, 16 * PAIRS + 1, 16) as landed:
                for v in range(SLOTS):
                    gathers(landed, v, t["x_nat"], s_idx, s_rows, (s_idx[v], 16))
            for v in range(NG - SLOTS * PAIRS):
                gathers(16 * (PAIRS + 1), v, t["x_nat"], s_idx, s_rows, (s_idx[v], 16))

            pool.wait_ge(s_xsw, 16 * NB)
            with pool.Fori(16, 16 * PAIRS + 1, 16) as landed:
                for v in range(SLOTS):
                    gathers(landed, v, x1s_table, s_idx2, s_rows2, (s_xsw, 16 * NB))
            for v in range(NG - SLOTS * PAIRS):
                gathers(16 * (PAIRS + 1), v, x1s_table, s_idx2, s_rows2, (s_xsw, 16 * NB))

        @block.tensor
        def _(pe):
            pe.wait_ge(s_const, N_CONST)
            pe.wait_ge(s_spread, 1)
            nc.tensor.matmul(ps_bn[:, 0:3 * NG + 1], ones[0:NG, :], spread[:, :], start=True, stop=True).then_inc(s_bcast, 1)

            def window(g, u, easy, lhs, rws, acc_sem, win_sem, far_hot_sem, far_win_sem):
                wait(pe, acc_sem, g - 1)
                for k in range(TG):
                    mm = nc.tensor.matmul(ps_win[u][0:rws, 0:W], lhs[:, k, :], hot[u][:, k, :],
                                          start=(k == 0), stop=(k == TG - 1))
                mm.then_inc(win_sem, 1)
                if easy:
                    return
                more = pe.value_load(steer[0:1, ds(NG + g, 1)], min_val=0, max_val=NW - 1)
                with pe.If(more > 0):
                    done = pe.value_load(steer[0:1, ds(2 * NG + g, 1)], min_val=0, max_val=NW * NG)
                    with pe.Fori(1, more + 1) as w:
                        pe.wait_ge(far_hot_sem, done + w)
                        for k in range(TG):
                            mm = nc.tensor.matmul(ps_win[u][0:rws, 0:W], lhs[:, k, :], far_hot[:, k, :],
                                                  start=(k == 0), stop=(k == TG - 1))
                        mm.then_inc(far_win_sem, 1)

            def window1(g, u, easy):
                pe.wait_ge(s_vals, g + 1)
                window(g, u, easy, vals[u], VC, s_acc, s_win, s_far_hot, s_far_win)

            def transposes(k, v):
                g = SLOTS * k + v
                pe.wait_ge(s_rows[v], 16 * TG * (k + 1))
                for m in range(TG):
                    if m % 4 == 0:
                        wait(pe, s_feat, 2 * g - 1 + m // 4)
                    mm = nc.tensor.transpose(ps_xt[m // 4][0:ND, P * (m % 4):P * (m % 4 + 1)], rows[v][:, m, :], ident[:, :])
                    if m % 4 == 3:
                        mm.then_inc(s_xt, 1)

            def step1(k, v, easy, b):
                g, u = SLOTS * k + v, v % 2
                if isinstance(g, int) and g == 0:
                    transposes(0, 0)
                if not (isinstance(g, int) and g == NG - 1):
                    transposes(k + (v + 1) // SLOTS, (v + 1) % SLOTS)
                beside = ([] if b is None else [None, lambda: block1b(b)] if u == 0 else
                          [lambda: agg(b, 2 * b + 3, b - 2), None, lambda: upd_in(b), lambda: upd_out(b)])
                for j, also in enumerate(spaced(beside)):
                    if j == 0:
                        if isinstance(g, int) and g == 0:
                            pe.wait_ge(s_w1, W1_LANDED)
                            pe.wait_ge(s_bias, 1)
                        pe.wait_ge(s_edge[u], 16 * (2 * k + v // 2 + 1))
                    if j % 2 == 0:
                        pe.wait_ge(s_feat, 2 * g + j // 2 + 1)
                    wait(pe, s_gelu, 4 * g + j - 1)
                    nc.tensor.matmul(ps_hid[j % 2][:, 0:2 * HC], ones_b[:, :], flat(b1_split[:, :, :]), start=True, stop=False)
                    for q in range(2):
                        m = 2 * j + q
                        mm = nc.tensor.matmul(ps_hid[j % 2][:, HC * q:HC * (q + 1)], feat[u][:, P * m:P * (m + 1)], w1[:, :],
                                              start=False, stop=(q == 1))
                    mm.then_inc(s_pre, 1)
                    if also is not None:
                        also()
                    if u == 0 and j == 0 and not (isinstance(g, int) and g == 0):
                        window1(g - 2, 0, easy)
                if u == 0 and not (isinstance(g, int) and g == 0):
                    window1(g - 1, 1, easy)

            def close1(easy):
                window1(NG - 2, 0, easy)
                window1(NG - 1, 1, easy)
                if not easy:
                    pe.wait_ge(s_acc, NG)

            def agg(b, added, copied):
                pe.wait_ge(s_acc, added)
                if isinstance(b, int) and b == 0:
                    pe.wait_ge(s_wts, WTS_LANDED)
                    pe.wait_ge(s_nodes, 32)
                    pe.wait_ge(s_fill, 1)
                wait(pe, s_xstc, copied)
                nc.tensor.matmul(ps_bt[0:ND, 0:P], mw2[:, :], acc1[0:ND + 1, ds(P * b, P)], start=True, stop=True).then_inc(s_agg, 1)

            def upd_in(b):
                pe.wait_ge(s_aggc, b + 1)
                nc.tensor.matmul(ps_bt[0:ND, P:2 * P], uw1x[:, :], x_t[:, ds(P * b, P)], start=True, stop=False)
                nc.tensor.matmul(ps_bt[0:ND, P:2 * P], uw1a[:, :], agg_t[:, :], start=False, stop=True).then_inc(s_upre, 1)
                wait(pe, s_updr, b)
                pe.wait_ge(s_wsum, b + 1)
                nc.tensor.matmul(ps_bn[:, ND:ND + 1], wsum[ND:VC, :], pick_w[ND:VC, :], start=True, stop=True)

            def upd_out(b):
                pe.wait_ge(s_ugelu, b + 1)
                nc.tensor.matmul(ps_bn[:, 0:ND], upd_t[:, :], uw2[:, :], start=True, stop=True).then_inc(s_upd, 1)

            def block1a(b):
                agg(b, all_added(b), b - 1)
                upd_in(b)
                upd_out(b)

            def block1b(b):
                wait(pe, s_xstc, b)
                pe.wait_ge(s_xs, b + 1)
                nc.tensor.transpose(ps_bt[0:ND, 2 * P:3 * P], xs[:, :], ident[:, :]).then_inc(s_xst, 1)

            run_pass(pe, step1, block1a, block1b, ahead=True, even=LAG + 3, odd=LAG, close=close1)

            def step2(k, v, easy, b):
                g, u = SLOTS * k + v, v % 2
                pe.wait_ge(s_rows2[v], 16 * TG * (k + 1))
                pe.wait_ge(s_hot2, g + 1)
                window(g, u, easy, rows[v], ND, s_acc2, s_win2[u], s_far_hot2, s_far_win2)
                if b is not None:
                    block2(b)

            def block2(b):
                pe.wait_ge(s_sum2, b + 1)
                wait(pe, s_finr, b)
                nc.tensor.matmul(ps_bn[:, 0:ND], agg_t[:, :], w_gcn[:, :], start=True, stop=True).then_inc(s_fin, 1)
            run_pass(pe, step2, block2, odd=LAG)

        @block.scalar
        def _(act):
            def copy_rows(g, u):
                for m in range(2):
                    act.wait_ge(s_xt, 2 * g + m + 1)
                    nc.scalar.activation(feat[u][0:ND, 4 * P * m:4 * P * (m + 1)], ps_xt[m][0:ND, :], ACT.Copy).then_inc(s_feat, 1)

            def step1(k, v, easy, b):
                g, u = SLOTS * k + v, v % 2
                if isinstance(g, int) and g == 0:
                    copy_rows(0, 0)
                if not (isinstance(g, int) and g == NG - 1):
                    copy_rows(g + 1, 1 - u)
                wait(act, s_vals, g - 1)
                beside = ([] if b is None else [None, lambda: block1b(b)] if u == 0 else
                          [lambda: copy_sums(b), None, lambda: upd_gelu(b)])
                for j, also in enumerate(spaced(beside)):
                    act.wait_ge(s_pre, 4 * g + j + 1)
                    nc.scalar.activation(flat(hid[u][:, 2 * j:2 * j + 2, :]), ps_hid[j % 2][:, 0:2 * HC], ACT.Gelu).then_inc(s_gelu, 1)
                    if j == SQUASH_AFTER[u] and not (isinstance(g, int) and g == 0):
                        squash1(g - 1, 1 - u)
                    if also is not None:
                        also()
                if not (isinstance(g, int) and g >= NG - 2):
                    act.dma_start(feat[u][ND:P, :], edge_view[:, ds(g + 2, 1), :].rearrange("p o c -> p (o c)")).then_inc(s_edge[u], 16)

            def squash1(g, u):
                act.wait_ge(s_logit, g + 1)
                nc.scalar.activation(squash[u][:, :], logit[u][:, :], ACT.Tanh, bias=half_gb2[:, :], scale=0.5).then_inc(s_squash, 1)

            def close1(easy):
                squash1(NG - 1, 1)

            def copy_sums(b):
                wait(act, s_upd, b)
                act.wait_ge(s_agg, b + 1)
                nc.scalar.activation(agg_t[:, :], ps_bt[0:ND, 0:P], ACT.Copy).then_inc(s_aggc, 1)
                nc.scalar.activation(wsum[ND:VC, :], acc1[ND:VC, ds(P * b, P)], ACT.Copy).then_inc(s_wsum, 1)

            def upd_gelu(b):
                act.wait_ge(s_upre, b + 1)
                nc.scalar.activation(upd_t[0:ND, :], ps_bt[0:ND, P:2 * P], ACT.Gelu).then_inc(s_ugelu, 1)

            def block1a(b):
                copy_sums(b)
                upd_gelu(b)

            def block1b(b):
                b = at(act, b)
                act.wait_ge(s_xs, b + 1)
                act.dma_start(x1s_view[:, ds(b, 1), :], xs[:, :].rearrange("p (o c) -> p o c", o=1)).then_inc(s_xsw, 16)
                act.wait_ge(s_xst, b + 1)
                nc.scalar.activation(acc2[:, ds(P * b, P)], ps_bt[0:ND, 2 * P:3 * P], ACT.Copy).then_inc(s_xstc, 1)
            run_pass(act, step1, block1a, block1b, ahead=True, even=LAG + 3, odd=LAG, close=close1)

            def step2(k, v, easy, b):
                if b is not None and v % 2:
                    block2(b, 2 * b + 3)
                elif b is not None:
                    block2b(b)

            def close2(easy):
                act.wait_ge(s_acc2, NG)

            def block2(b, added):
                act.wait_ge(s_acc2, added)
                wait(act, s_fin, b)
                nc.scalar.activation(agg_t[:, :], acc2[:, ds(P * b, P)], ACT.Copy).then_inc(s_sum2, 1)

            def block2b(b):
                b = at(act, b)
                act.wait_ge(s_y, b + 1)
                act.dma_start(out_view[:, ds(b, 1), :], y[:, :].rearrange("p (o c) -> p o c", o=1)).then_inc(s_out, 16)
            run_pass(act, step2, lambda b: block2(b, all_added(b)), block2b, even=LAG + 1, odd=LAG, close=close2)
            act.wait_ge(s_out, 16 * NB)

        @block.vector
        def _(dve):
            nc.vector.memset(b1_split[:, :, :], 0.0)
            nc.vector.memset(acc2[:, NP:AW], 0.0)
            nc.vector.memset(rin[:, :], 1.0)
            nc.vector.memset(upd_t[ND:ND + 1, :], 1.0).then_inc(s_fill, 1)

            chain = [0]

            def link(ins):
                chain[0] += 1
                ins.then_inc(s_chain, 1)
                dve.wait_ge(s_chain, chain[0])

            dve.wait_ge(s_win_in, 16)
            nc.vector.tensor_reduce(lo[:, :], dst_rows[:, :], AX, ALU.min)
            link(nc.vector.tensor_reduce(hi[:, :], dst_rows[:, :], AX, ALU.max))
            link(nc.vector.tensor_tensor(reach[:, :], hi[:, :], lo[:, :], ALU.subtract))
            dve.wait_ge(s_const, N_CONST)
            nc.vector.tensor_copy(iota_w[:, :], iota_i[:, :])
            nc.vector.tensor_copy(due[:, :], due_i[:, :])
            link(nc.vector.tensor_copy(win_off[:, :], win_i[:, :]))
            link(nc.vector.tensor_scalar(crossed[:, 1:NW], win_off[0:NG, 1:NW], reach[:, :], None, ALU.is_le))
            link(nc.vector.tensor_reduce(extra[:, :], crossed[:, 1:NW], AX, ALU.add))
            nc.vector.tensor_scalar(spread[:, 0:NG], ident[0:NG, 0:NG], lo[:, :], None, ALU.mult)
            nc.vector.tensor_scalar(spread[:, NG:2 * NG], ident[0:NG, 0:NG], extra[:, :], None, ALU.mult)
            nc.vector.scalar_tensor_tensor(spread[:, 3 * NG:3 * NG + 1], lo[:, :], due[0:NG, :], extra[:, :],
                                           ALU.is_lt, ALU.add)
            nc.vector.tensor_scalar(spread[:, 2 * NG:3 * NG], before[0:NG, :], extra[:, :], None, ALU.mult).then_inc(s_spread, 1)
            dve.wait_ge(s_bcast, 1)
            nc.vector.tensor_copy(steer[0:1, :], ps_bn[0:1, 0:3 * NG + 1])
            link(nc.vector.tensor_copy(lo_all[:, :], ps_bn[:, 0:NG]))
            dve.wait_ge(s_dst, 32)
            link(nc.vector.tensor_tensor(dst_rel[:, :].rearrange("p (g k) -> p g k", k=TG),
                                         dst_i[:, :].rearrange("p (g k) -> p g k", k=TG),
                                         lo_all[:, :].rearrange("p (g o) -> p g o", o=1).to_broadcast([P, NG, TG]),
                                         ALU.subtract))
            dve.wait_ge(s_w1, W1_LANDED)
            rest = b1
            for k in range(3):
                link(nc.vector.tensor_copy(b1_hi[:, :, :], rest[:, :, :]))
                link(nc.vector.tensor_scalar(b1_part[:, :, :], b1_hi[:, :, :], ident[0:3, k:k + 1], None, ALU.mult))
                if k == 0:
                    link(nc.vector.tensor_copy(b1_sum[:, :, :], b1_part[:, :, :]))
                else:
                    link(nc.vector.tensor_tensor(b1_sum[:, :, :], b1_sum[:, :, :], b1_part[:, :, :], ALU.add))
                link(nc.vector.tensor_tensor(b1_rest[:, :, :], rest[:, :, :], b1_hi[:, :, :], ALU.subtract))
                rest = b1_rest
            link(nc.vector.tensor_copy(b1_split[0:3, :, :], b1_sum[:, :, :]))
            nc.vector.memset(step[:, 0:1], 0.0).then_inc(s_bias, 1)
            dve.wait_ge(s_wts, WTS_LANDED)
            link(nc.vector.tensor_scalar(half_gb2[:, :], gb2[:, :], 0.5, None, ALU.mult))
            nc.vector.memset(step[:, 1:2], 0.0).then_inc(s_steer, 1)
            nc.vector.memset(acc1[:, :], 0.0)

            def over_window(ap):
                return ap.rearrange("p (k o) -> p k o", o=1).to_broadcast([P, TG, W])

            def one_hot(place, rel):
                return nc.vector.tensor_tensor(
                    place[:, :, :], over_window(rel),
                    iota_w[:, :].rearrange("p (o w) -> p o w", o=1).to_broadcast([P, TG, W]), ALU.is_equal)

            def weigh_hot(place, g):
                return nc.vector.tensor_tensor(place[:, :, :], place[:, :, :], over_window(weight[:, ds(TG * g, TG)]), ALU.mult)

            def take_window(acc, rws, g, u, easy, win_sem, win_count, acc_sem, far_hot_sem, far_win_sem, weigh):
                first_node = dve.value_load(steer[0:1, ds(g, 1)], min_val=0, max_val=NP - 1)
                nc.vector.drain()
                dve.wait_ge(win_sem, win_count)
                added = nc.vector.tensor_tensor(acc[0:rws, ds(first_node, W)], acc[0:rws, ds(first_node, W)],
                                                ps_win[u][0:rws, 0:W], ALU.add)
                if easy:
                    added.then_inc(acc_sem, 1)
                    return
                more = dve.value_load(steer[0:1, ds(NG + g, 1)], min_val=0, max_val=NW - 1)
                with dve.If(more > 0):
                    done = dve.value_load(steer[0:1, ds(2 * NG + g, 1)], min_val=0, max_val=NW * NG)
                    with dve.Fori(1, more + 1) as w:
                        nc.vector.drain()
                        nc.vector.tensor_scalar(far_rel[:, :], dst_rel[:, ds(TG * g, TG)], win_off[:, ds(w, 1)], None,
                                                ALU.subtract)
                        nc.vector.drain()
                        if weigh:
                            one_hot(far_hot, far_rel[:, :])
                            nc.vector.drain()
                            weigh_hot(far_hot, g).then_inc(far_hot_sem, 1)
                        else:
                            one_hot(far_hot, far_rel[:, :]).then_inc(far_hot_sem, 1)
                        dve.wait_ge(far_win_sem, done + w)
                        node = nc.s_assert_within(dve.snap(first_node + w * W), 0, AW - W)
                        nc.vector.tensor_tensor(acc[0:rws, ds(node, W)], acc[0:rws, ds(node, W)],
                                                ps_win[u][0:rws, 0:W], ALU.add)
                nc.vector.drain()
                nc.vector.memset(far_rel[:, 0:1], 0.0).then_inc(acc_sem, 1)

            def rsqrt(a, z):
                v, r, s = rin[:, a:z], root[:, a:z], step[:, a:z]
                nc.vector.drain()
                nc.vector.tensor_scalar(s.bitcast(i32), v.bitcast(i32), 1, None, ALU.logical_shift_right)
                nc.vector.drain()
                nc.vector.tensor_scalar(r.bitcast(i32), s.bitcast(i32), -1.0, ROOT_SEED, ALU.mult, ALU.add)
                for _ in range(3):
                    nc.vector.drain()
                    nc.vector.scalar_tensor_tensor(s, r, -0.5, r, ALU.mult, ALU.mult)
                    nc.vector.drain()
                    nc.vector.tensor_tensor(s, s, v, ALU.mult)
                    nc.vector.drain()
                    nc.vector.scalar_tensor_tensor(r, s, 1.5, r, ALU.add, ALU.mult)
                nc.vector.drain()

            def window1(g, u, easy):
                take_window(acc1, VC, g, u, easy, s_win, g + 1, s_acc, s_far_hot, s_far_win, False)

            def gate1(g, u):
                dve.wait_ge(s_squash, g + 1)
                nc.vector.tensor_scalar(vals[u][:, :, ND:ND + 1], squash[u][:, :].rearrange("p (k o) -> p k o", o=1),
                                        0.5, 0.5, ALU.mult, ALU.add)
                nc.vector.drain()
                nc.vector.tensor_tensor(vals[u][:, :, 0:ND], hid[u][:, :, 0:ND],
                                        vals[u][:, :, ND:ND + 1].to_broadcast([P, TG, ND]), ALU.mult).then_inc(s_vals, 1)

            def step1(k, v, easy, b):
                g, u = SLOTS * k + v, v % 2
                if u == 0 and not (isinstance(g, int) and g == 0):
                    gate1(g - 1, 1)
                if not (isinstance(g, int) and g < 2):
                    window1(g - 2, u, easy)
                one_hot(hot[u], dst_rel[:, ds(TG * g, TG)])
                nc.vector.tensor_copy(vals[u][:, :, ND + 1:VC], weight[:, ds(TG * g, TG)].rearrange("p (k o) -> p k o", o=1))
                if u == 1:
                    gate1(g - 1, 0)
                if b is not None:
                    block1a(b)
                dve.wait_ge(s_gelu, 4 * g + 4)
                nc.vector.tensor_tensor(prod[:, :, :], hid[u][:, :, ND:HC],
                                        gw2[:, :].rearrange("p (o c) -> p o c", o=1).to_broadcast([P, TG, ND]), ALU.mult)
                nc.vector.drain()
                nc.vector.tensor_reduce(logit[u][:, :], prod[:, :, :], AX, ALU.add).then_inc(s_logit, 1)

            def close1(easy):
                gate1(NG - 1, 1)
                window1(NG - 2, 0, easy)
                window1(NG - 1, 1, easy)

            def block1(b, first, second):
                here, last = ds(b, 1), ds(b - 1, 1)
                row = lambda a, where: a[:, where, :].rearrange("p o c -> p (o c)")
                nc.vector.drain()
                if second:
                    nc.vector.bn_stats(stats[:, 1, :], h2[:, :])
                if first:
                    if isinstance(b, int) and b == 0:
                        dve.wait_ge(s_nodes, 32)
                    dve.wait_ge(s_upd, b + 1)
                    nc.vector.tensor_tensor(h[:, :], row(x_nat, here), ps_bn[:, 0:ND], ALU.add)
                    nc.vector.tensor_scalar(deg[:, :], ps_bn[:, ND:ND + 1], 1.0, 0.0, ALU.add, ALU.is_gt)
                    nc.vector.tensor_scalar(rin[:, 2:3], ps_bn[:, ND:ND + 1], 1.0, 1e-30, ALU.add, ALU.max).then_inc(s_updr, 1)
                    nc.vector.tensor_tensor(row(x1b, here), row(x_nat, here), ln_b[:, :], ALU.add)
                    nc.vector.drain()
                    nc.vector.bn_stats(stats[:, 0, :], h[:, :])
                nc.vector.drain()
                if first:
                    nc.vector.bn_aggr(mv[:, 0, :], stats[:, 0, :])
                if second:
                    nc.vector.bn_aggr(mv[:, 1, :], stats[:, 1, :])
                nc.vector.drain()
                lo_col, hi_col = (0 if first else 1), (2 if second else 1)
                nc.vector.tensor_scalar(rin[:, lo_col:hi_col].rearrange("p (k o) -> p k o", o=1),
                                        mv[:, lo_col:hi_col, 1:2], EPS, None, ALU.add)
                if first:
                    nc.vector.scalar_tensor_tensor(h_g[:, :], h[:, :], mv[:, 0, 0:1], ln_g[:, :], ALU.subtract, ALU.mult)
                if second:
                    nc.vector.tensor_scalar(h2_c[:, :], h2[:, :], mv[:, 1, 0:1], None, ALU.subtract)
                rsqrt(lo_col, 3 if first else 2)
                if second:
                    wait(dve, s_xst, b - 1)
                    wait(dve, s_xsw, 16 * b - 16)
                    nc.vector.tensor_scalar(xs[:, :], h2_c[:, :], root[:, 1:2], dinv[:, last], ALU.mult,
                                            ALU.mult).then_inc(s_xs, 1)
                    nc.vector.scalar_tensor_tensor(row(x1b, last), h2_c[:, :], root[:, 1:2], b_gcn[:, :], ALU.mult, ALU.add)
                if first:
                    nc.vector.tensor_tensor(dinv[:, here], root[:, 2:3], deg[:, :], ALU.mult)
                    nc.vector.scalar_tensor_tensor(h2[:, :], h_g[:, :], root[:, 0:1], row(x1b, here), ALU.mult, ALU.add)

            def block1a(b):
                block1(b, True, not (isinstance(b, int) and b == 0))

            def finish1():
                block1(NB, False, True)
            run_pass(dve, step1, block1a, ahead=True, even=LAG + 1, close=close1, finish=finish1)
            dve.wait_ge(s_xstc, NB)

            def step2(k, v, easy, b):
                g, u = SLOTS * k + v, v % 2
                one_hot(hot[u], dst_rel[:, ds(TG * g, TG)])
                nc.vector.drain()
                weigh_hot(hot[u], g).then_inc(s_hot2, 1)
                if not (isinstance(g, int) and g == 0):
                    take_window(acc2, ND, g - 1, 1 - u, easy, s_win2[1 - u], 2 * k + v // 2 + u, s_acc2, s_far_hot2, s_far_win2, True)
                if b is not None:
                    block2(b)

            def close2(easy):
                take_window(acc2, ND, NG - 1, 1, easy, s_win2[1], TURNS, s_acc2, s_far_hot2, s_far_win2, True)

            def block2(b):
                here = ds(b, 1)
                nc.vector.drain()
                dve.wait_ge(s_fin, b + 1)
                nc.vector.scalar_tensor_tensor(h[:, :], ps_bn[:, 0:ND], dinv[:, here], x1b[:, here, :].rearrange("p o c -> p (o c)"),
                                               ALU.mult, ALU.add).then_inc(s_finr, 1)
                nc.vector.drain()
                nc.vector.bn_stats(stats[:, 0, :], h[:, :])
                nc.vector.drain()
                nc.vector.bn_aggr(mv[:, 0, :], stats[:, 0, :])
                nc.vector.drain()
                nc.vector.tensor_scalar(rin[:, 0:1], mv[:, 0, 1:2], EPS, None, ALU.add)
                rsqrt(0, 1)
                wait(dve, s_out, 16 * b)
                nc.vector.tensor_scalar(y[:, :], h[:, :], mv[:, 0, 0:1], root[:, 0:1], ALU.subtract, ALU.mult).then_inc(s_y, 1)
            run_pass(dve, step2, block2, odd=LAG, close=close2)


N_CONST = 9


def kernel(**inputs):
    import numpy as np
    import concourse.bacc as bacc
    from concourse import mybir as mb
    from concourse.bass_utils import run_bass_kernel_spmd

    a = {k.replace("L0_gnn_", "").replace("L1_gnn_", ""): np.asarray(v) for k, v in inputs.items()}
    EPAD = NT * P

    def by_tile(v, fill):
        full = np.full((EPAD,), fill, v.dtype)
        full[:E] = v
        return full.reshape(NT, P).T

    x = np.zeros((NP, ND), np.float32)
    x[:N] = a["x"]
    edge = np.zeros((EPAD, ED), np.float32)
    edge[:E] = a["edge_attr_32"]
    dst = np.full((EPAD,), N, np.int32)
    dst[:E] = a["dst"]
    rep = lambda v, n=P: np.broadcast_to(v.reshape(1, -1), (n, v.size))
    arrays = {
        "x_t": np.concatenate([x.T, np.ones((1, NP), np.float32)]),
        "x_nat": x,
        "src_t": by_tile(a["src"].astype(np.int32), 0),
        "dst_t": by_tile(a["dst"].astype(np.int32), N),
        "dst_rows": dst.reshape(NG, GE),
        "weight_t": by_tile(a["edge_weight"], 0),
        "edge_t": edge.T,
        "mW1": a["mW1"], "gW1": a["gW1"], "mb1_3": rep(a["mb1"], 3), "gb1_3": rep(a["gb1"], 3),
        "gW2": rep(a["gW2"]), "gb2": rep(a["gb2"]),
        "mW2": a["mW2"], "mb2": a["mb2"].reshape(1, ND),
        "uW1": a["uW1"], "ub1": a["ub1"].reshape(1, ND), "uW2": a["uW2"], "ub2": a["ub2"].reshape(1, ND),
        "W": a["W"], "ln_g": rep(a["ln_g"]), "ln_b": rep(a["ln_b"]), "b": rep(a["b"]),
    }
    arrays = {f"in_{k}": np.ascontiguousarray(v) for k, v in arrays.items()}
    nc = bacc.Bacc("TRN2", target_bir_lowering=False, num_devices=1)
    t = {k[3:]: nc.dram_tensor(k, v.shape, mb.dt.from_np(v.dtype), kind="ExternalInput").ap() for k, v in arrays.items()}
    out = nc.dram_tensor("out_nodes", (NP, ND), mb.dt.float32, kind="ExternalOutput").ap()
    gnn_kernel(nc, t, out)
    r = run_bass_kernel_spmd(nc, [arrays], core_ids=[0])
    return r.results[0]["out_nodes"][:N]
```

```python
import concourse.bass as bass
from concourse import mybir
from contextlib import ExitStack

P = 128
N, E = 6250, 100000
ND, ED = 96, 32
TG = 8
GE = TG * P
TURNS = -(-E // (2 * GE))
NG = 2 * TURNS
NT = NG * TG
NB = -(-N // P)
NP = NB * P
W = 80
NW = -(-NP // W)
AW = NP + 2 * W
VC = ND + 2
HC = 2 * ND
SLOTS = 4
PAIRS = TURNS // 2
PEELED = 3
LAG = 2
LAST = 4
REST = NT - -(-E // P)
SQUASH_AFTER = (0, 3)
N_CONST = 9
EPS = 1e-5
ROOT_SEED = float(0x5F3759DF)
assert ND + ED == P and NB == TURNS == 2 * PAIRS + 1


def gnn_kernel(nc, t, out):
    fp32, i32, bf16 = mybir.dt.float32, mybir.dt.int32, mybir.dt.bfloat16
    ALU = mybir.AluOpType
    ACT = mybir.ActivationFunctionType
    AX = mybir.AxisListType.X
    ds = bass.ds

    x1s_table = nc.dram_tensor("x1s_table", [NP, ND], fp32, kind="Internal").ap()

    ctx = ExitStack()
    with ctx:
        def sb(name, shape, dt=fp32):
            return ctx.enter_context(nc.sbuf_tensor(name, shape, dt))

        def sem(name):
            return ctx.enter_context(nc.semaphore(name))

        ident = sb("ident", [P, P])
        before = sb("before", [P, NG])
        ones = sb("ones", [P, P])
        ones_b = sb("ones_b", [P, P], bf16)
        iota_w = sb("iota_w", [P, W])
        iota_i = sb("iota_i", [P, W], i32)
        win_i = sb("win_i", [P, NW], i32)
        win_off = sb("win_off", [P, NW])
        due_i = sb("due_i", [P, 1], i32)
        due = sb("due", [P, 1])
        pick_w = sb("pick_w", [P, 1])
        w1 = sb("w1", [P, HC])
        b1 = sb("b1", [3, 2, HC])
        b1_rest = sb("b1_rest", [3, 2, HC])
        b1_part = sb("b1_part", [3, 2, HC])
        b1_sum = sb("b1_sum", [3, 2, HC])
        b1_hi = sb("b1_hi", [3, 2, HC], bf16)
        b1_split = sb("b1_split", [P, 2, HC], bf16)
        gw2 = sb("gw2", [P, ND])
        gb2 = sb("gb2", [P, 1])
        half_gb2 = sb("half_gb2", [P, 1])
        mw2 = sb("mw2", [ND + 1, ND])
        uw1x = sb("uw1x", [ND + 1, ND])
        uw1a = sb("uw1a", [ND, ND])
        uw2 = sb("uw2", [ND + 1, ND])
        w_gcn = sb("w_gcn", [ND, ND])
        ln_g = sb("ln_g", [P, ND])
        ln_b = sb("ln_b", [P, ND])
        b_gcn = sb("b_gcn", [P, ND])
        dst_rows = sb("dst_rows", [NG, GE], i32)
        lo = sb("lo", [NG, 1])
        hi = sb("hi", [NG, 1])
        reach = sb("reach", [NG, 1])
        crossed = sb("crossed", [NG, NW])
        extra = sb("extra", [NG, 1])
        spread = sb("spread", [NG, 3 * NG + 1])
        lo_all = sb("lo_all", [P, NG])
        steer = sb("steer", [1, 3 * NG + 1], i32)
        dst_i = sb("dst_i", [P, NT], i32)
        dst_rel = sb("dst_rel", [P, NT])
        weight = sb("weight", [P, NT])
        x_t = sb("x_t", [ND + 1, NP])
        x_nat = sb("x_nat", [P, NB, ND])
        x1b = sb("x1b", [P, NB, ND])
        dinv = sb("dinv", [P, NB])
        acc1 = sb("acc1", [VC, AW])
        acc2 = sb("acc2", [ND, AW])
        idx = [sb(f"idx{v}", [P, TG], i32) for v in range(SLOTS)]
        rows = [sb(f"rows{v}", [P, TG, ND]) for v in range(SLOTS)]
        feat = [sb(f"feat{u}", [P, GE]) for u in range(2)]
        hid = [sb(f"hid{u}", [P, TG, HC]) for u in range(2)]
        vals = [sb(f"vals{u}", [P, TG, VC]) for u in range(2)]
        hot = [sb(f"hot{u}", [P, TG, W]) for u in range(2)]
        logit = [sb(f"logit{u}", [P, TG]) for u in range(2)]
        squash = [sb(f"squash{u}", [P, TG]) for u in range(2)]
        prod = sb("prod", [P, TG, ND])
        far_rel = sb("far_rel", [P, TG])
        far_hot = sb("far_hot", [P, TG, W])
        agg_t = sb("agg_t", [ND, 2 * P])
        upd_t = sb("upd_t", [ND + 1, 2 * P])
        wsum = sb("wsum", [P, 2 * P])
        h = sb("h", [P, LAST, ND])
        h_g = sb("h_g", [P, LAST, ND])
        h2 = sb("h2", [P, LAST, ND])
        h2_c = sb("h2_c", [P, LAST, ND])
        xs = sb("xs", [P, LAST, ND])
        y = sb("y", [P, 2, ND])
        stats = sb("stats", [P, LAST + 1, 6])
        mv = sb("mv", [P, LAST + 1, 2])
        rin = sb("rin", [P, 2 * LAST + 1])
        root = sb("root", [P, 2 * LAST + 1])
        step = sb("step", [P, 2 * LAST + 1])
        deg = sb("deg", [P, LAST])

        def psum(name):
            return ctx.enter_context(nc.psum_tensor(name, [P, 512], fp32))

        ps_xt = [psum(f"ps_xt{k}") for k in range(2)]
        ps_hid = [psum(f"ps_hid{k}") for k in range(2)]
        ps_win = [psum(f"ps_win{k}") for k in range(2)]
        ps_bt = psum("ps_bt")
        ps_bn = psum("ps_bn")

        s_win_in = sem("s_win_in")
        s_dst = sem("s_dst")
        s_w1 = sem("s_w1")
        s_wts = sem("s_wts")
        s_nodes = sem("s_nodes")
        s_const = sem("s_const")
        s_fill = sem("s_fill")
        s_chain = sem("s_chain")
        s_spread = sem("s_spread")
        s_bcast = sem("s_bcast")
        s_steer = sem("s_steer")
        s_bias = sem("s_bias")
        s_idx = [sem(f"s_idx{v}") for v in range(SLOTS)]
        s_edge = [sem(f"s_edge{u}") for u in range(2)]
        s_rows = [sem(f"s_rows{v}") for v in range(SLOTS)]
        s_xt = sem("s_xt")
        s_feat = sem("s_feat")
        s_pre = sem("s_pre")
        s_gelu = sem("s_gelu")
        s_logit = sem("s_logit")
        s_squash = sem("s_squash")
        s_vals = sem("s_vals")
        s_win = sem("s_win")
        s_acc = sem("s_acc")
        s_far_hot = sem("s_far_hot")
        s_far_win = sem("s_far_win")
        s_wsum = sem("s_wsum")
        s_agg = sem("s_agg")
        s_aggc = sem("s_aggc")
        s_upre = sem("s_upre")
        s_ugelu = sem("s_ugelu")
        s_upd = sem("s_upd")
        s_updr = sem("s_updr")
        s_xs = sem("s_xs")
        s_xst = sem("s_xst")
        s_xstc = sem("s_xstc")
        s_xsw = sem("s_xsw")
        s_idx2 = [sem(f"s_idx2{v}") for v in range(SLOTS)]
        s_rows2 = [sem(f"s_rows2{v}") for v in range(SLOTS)]
        s_hot2 = sem("s_hot2")
        s_win2 = [sem(f"s_win2{u}") for u in range(2)]
        s_acc2 = sem("s_acc2")
        s_far_hot2 = sem("s_far_hot2")
        s_far_win2 = sem("s_far_win2")
        s_sum2 = sem("s_sum2")
        s_fin = sem("s_fin")
        s_finr = sem("s_finr")
        s_y = sem("s_y")
        s_out = sem("s_out")

        def at(eng, place):
            return place if isinstance(place, int) else eng.snap(place)

        def wait(eng, s, count):
            if not isinstance(count, int) or count > 0:
                eng.wait_ge(s, count)

        def run_pass(eng, step_fn, block_a=None, block_b=None, even=None, odd=None, ahead=False, end=None, close=None, finish=None):
            def second_part(b):
                if block_b is not None:
                    block_b(b)

            def turn(k, q, easy):
                i = 2 * k + q

                def beside(lag):
                    return None if not easy or lag is None or (isinstance(i, int) and i < lag) else i - lag

                if not (ahead and isinstance(i, int) and i == 0):
                    step_fn(k, 2 * q, easy, beside(even))
                step_fn(k, 2 * q + 1, easy, beside(odd))

            if ahead:
                step_fn(0, 0, True, None)
                eng.wait_ge(s_steer, 1)
            hard = eng.value_load(steer[0:1, 3 * NG:3 * NG + 1], min_val=0, max_val=NG * NW)
            with eng.If(hard < 1):
                for i in range(2 * PEELED):
                    turn(i // 2, i % 2, True)
                with eng.Fori(PEELED, PAIRS) as k:
                    turn(k, 0, True)
                    turn(k, 1, True)
                turn(PAIRS, 0, True)
                if end is not None:
                    end()
            with eng.Else():
                turn(0, 0, False)
                turn(0, 1, False)
                with eng.Fori(1, PAIRS) as k:
                    turn(k, 0, False)
                    turn(k, 1, False)
                turn(PAIRS, 0, False)
                if close is not None:
                    close()
                if block_a is not None:
                    block_a(0)
                    with eng.Fori(1, NB) as b:
                        block_a(b)
                        second_part(b - 1)
                    second_part(NB - 1)
                if finish is not None:
                    finish()

        def group_rows(k, v):
            last = isinstance(k, int) and SLOTS * k + v == NG - 1
            return 16 * (TG * (k + 1) - (REST if last else 0))

        def spaced(items):
            return items + [None] * (TG // 2 - len(items))

        src_view = t["src_t"].rearrange("p (g c) -> p g c", g=NG)
        edge_view = t["edge_t"].rearrange("f (g c) -> f g c", g=NG)
        x1s_view = x1s_table.rearrange("(b p) c -> p b c", p=P)
        out_view = out.rearrange("(b p) c -> p b c", p=P)

        def flat(ap):
            return ap.rearrange("p a b -> p (a b)")

        WTS = [(w1[:, 0:ND], t["mW1"]), (w1[:, ND:HC], t["gW1"]),
               (b1[:, 0, 0:ND], t["mb1_3"]), (b1[:, 0, ND:HC], t["gb1_3"]),
               (b1[:, 1, 0:ND], t["mb1_3"]), (b1[:, 1, ND:HC], t["gb1_3"]),
               (gw2[:, :], t["gW2"]), (gb2[:, :], t["gb2"]),
               (mw2[0:ND, :], t["mW2"]), (mw2[ND:ND + 1, :], t["mb2"]),
               (uw1x[0:ND, :], t["uW1"][0:ND, :]), (uw1x[ND:ND + 1, :], t["ub1"]),
               (uw1a[:, :], t["uW1"][ND:HC, :]),
               (uw2[0:ND, :], t["uW2"]), (uw2[ND:ND + 1, :], t["ub2"]),
               (w_gcn[:, :], t["W"]), (ln_g[:, :], t["ln_g"]), (ln_b[:, :], t["ln_b"]),
               (b_gcn[:, :], t["b"])]
        N_W1 = 6
        W1_LANDED, WTS_LANDED = 16 * N_W1, 16 * (len(WTS) - N_W1)

        block = ctx.enter_context(nc.Block())

        @block.sync
        def _(sp):
            def load_idx(g, v, sems):
                sp.dma_start(idx[v][:, :], src_view[:, ds(g, 1), :].rearrange("p o c -> p (o c)")).then_inc(sems[v], 16)

            def load1(k, v, easy, b):
                if isinstance(k, int) and k == 0:
                    return
                g = at(sp, SLOTS * k + v)
                sp.wait_ge(s_xt, 2 * g - 6)
                load_idx(g, v, s_idx)

            load_idx(0, 0, s_idx)
            load_idx(1, 1, s_idx)
            sp.dma_start(dst_rows[:, :], t["dst_rows"]).then_inc(s_win_in, 16)
            sp.dma_start(feat[0][ND:P, :], edge_view[:, 0, :]).then_inc(s_edge[0], 16)
            for dst, src in WTS[:N_W1]:
                sp.dma_start(dst, src).then_inc(s_w1, 16)
            load_idx(2, 2, s_idx)
            load_idx(3, 3, s_idx)
            sp.dma_start(dst_i[:, :], t["dst_t"]).then_inc(s_dst, 16)
            sp.dma_start(weight[:, :], t["weight_t"]).then_inc(s_dst, 16)
            for dst, src in WTS[N_W1:]:
                sp.dma_start(dst, src).then_inc(s_wts, 16)
            sp.dma_start(feat[1][ND:P, :], edge_view[:, 1, :]).then_inc(s_edge[1], 16)
            sp.dma_start(x_t[:, :], t["x_t"]).then_inc(s_nodes, 16)
            sp.dma_start(x_nat[:, :, :], t["x_nat"].rearrange("(b p) c -> p b c", p=P)).then_inc(s_nodes, 16)

            def end1():
                for m in range(1, LAST, 2):
                    sp.wait_ge(s_xs, NB - LAST + m + 1)
                    sp.dma_start(x1s_view[:, NB - LAST + m, :], xs[:, m, :]).then_inc(s_xsw, 16)
            run_pass(sp, load1, ahead=True, end=end1)

            def load2(k, v, easy, b):
                g = at(sp, SLOTS * k + v)
                if isinstance(k, int) and k == 0:
                    sp.wait_ge(s_xt, 2 * (NG - (NG - 1 - v) % SLOTS))
                elif easy:
                    sp.wait_ge(s_win2[v % 2], 2 * k + v // 2 - 1)
                else:
                    sp.wait_ge(s_acc2, g - 3)
                load_idx(g, v, s_idx2)

            def end2():
                sp.wait_ge(s_y, NB)
                sp.dma_start(out_view[:, NB - 1, :], y[:, 1, :]).then_inc(s_out, 16)
            run_pass(sp, load2, end=end2)

        @block.gpsimd
        def _(pool):
            def gathers(landed, v, table, idx_sem, rows_sem, known):
                pool.wait_ge(*known)
                pool.wait_ge(idx_sem[v], landed)
                last = isinstance(landed, int) and landed == 16 * (PAIRS + 1) and v == (NG - 1) % SLOTS
                for k in range(TG - (REST if last else 0)):
                    nc.gpsimd.indirect_dma_start(
                        out=rows[v][:, k, :], out_offset=None, in_=table,
                        in_offset=bass.IndirectOffsetOnAxis(ap=idx[v][:, k:k + 1], axis=0)).then_inc(rows_sem[v], 16)

            def const(ins):
                ins.then_inc(s_const, 1)
                return 1
            n_const = 0
            gathers(16, 0, t["x_nat"], s_idx, s_rows, (s_idx[0], 16))
            n_const += const(nc.gpsimd.memset(ident[:, :], 0.0))
            n_const += const(nc.gpsimd.memset(ones[:, :], 1.0))
            n_const += const(nc.gpsimd.memset(ones_b[:, :], 1.0))
            n_const += const(nc.gpsimd.iota(iota_i[:, :], [[1, W]], base=0, channel_multiplier=0))
            n_const += const(nc.gpsimd.iota(win_i[:, :], [[W, NW]], base=0, channel_multiplier=0))
            n_const += const(nc.gpsimd.iota(due_i[:, :], [[0, 1]], base=-P // 2, channel_multiplier=P // 2))
            pool.wait_ge(s_const, n_const)
            n_const += const(nc.gpsimd.affine_select(out=ident[:, :], in_=ident[:, :], compare_op=ALU.not_equal, fill=1.0,
                                                     base=0, pattern=[[-1, P]], channel_multiplier=1))
            n_const += const(nc.gpsimd.affine_select(out=before[:, :], in_=ones[:, 0:NG], compare_op=ALU.is_gt, fill=0.0,
                                                     base=0, pattern=[[1, NG]], channel_multiplier=-1))
            n_const += const(nc.gpsimd.affine_select(out=pick_w[:, :], in_=ones[:, 0:1], compare_op=ALU.is_gt, fill=0.0,
                                                     base=-ND, pattern=[[0, 1]], channel_multiplier=1))
            assert n_const == N_CONST
            for v in range(1, SLOTS):
                gathers(16, v, t["x_nat"], s_idx, s_rows, (s_idx[v], 16))
            with pool.Fori(32, 16 * PAIRS + 1, 16) as landed:
                for v in range(SLOTS):
                    gathers(landed, v, t["x_nat"], s_idx, s_rows, (s_idx[v], 16))
            for v in range(NG - SLOTS * PAIRS):
                gathers(16 * (PAIRS + 1), v, t["x_nat"], s_idx, s_rows, (s_idx[v], 16))

            pool.wait_ge(s_xsw, 16 * NB)
            with pool.Fori(16, 16 * PAIRS + 1, 16) as landed:
                for v in range(SLOTS):
                    gathers(landed, v, x1s_table, s_idx2, s_rows2, (s_xsw, 16 * NB))
            for v in range(NG - SLOTS * PAIRS):
                gathers(16 * (PAIRS + 1), v, x1s_table, s_idx2, s_rows2, (s_xsw, 16 * NB))

        @block.tensor
        def _(pe):
            pe.wait_ge(s_const, N_CONST)
            pe.wait_ge(s_spread, 1)
            nc.tensor.matmul(ps_bn[:, 0:3 * NG + 1], ones[0:NG, :], spread[:, :], start=True, stop=True).then_inc(s_bcast, 1)

            def window(g, u, easy, lhs, rws, acc_sem, win_sem, far_hot_sem, far_win_sem):
                wait(pe, acc_sem, g - 1)
                for k in range(TG):
                    mm = nc.tensor.matmul(ps_win[u][0:rws, 0:W], lhs[:, k, :], hot[u][:, k, :],
                                          start=(k == 0), stop=(k == TG - 1))
                mm.then_inc(win_sem, 1)
                if easy:
                    return
                more = pe.value_load(steer[0:1, ds(NG + g, 1)], min_val=0, max_val=NW - 1)
                with pe.If(more > 0):
                    done = pe.value_load(steer[0:1, ds(2 * NG + g, 1)], min_val=0, max_val=NW * NG)
                    with pe.Fori(1, more + 1) as w:
                        pe.wait_ge(far_hot_sem, done + w)
                        for k in range(TG):
                            mm = nc.tensor.matmul(ps_win[u][0:rws, 0:W], lhs[:, k, :], far_hot[:, k, :],
                                                  start=(k == 0), stop=(k == TG - 1))
                        mm.then_inc(far_win_sem, 1)

            def window1(g, u, easy):
                pe.wait_ge(s_vals, g + 1)
                window(g, u, easy, vals[u], VC, s_acc, s_win, s_far_hot, s_far_win)

            def transposes(k, v):
                g = SLOTS * k + v
                pe.wait_ge(s_rows[v], group_rows(k, v))
                for m in range(TG):
                    if m % 4 == 0:
                        wait(pe, s_feat, 2 * g - 1 + m // 4)
                    mm = nc.tensor.transpose(ps_xt[m // 4][0:ND, P * (m % 4):P * (m % 4 + 1)], rows[v][:, m, :], ident[:, :])
                    if m % 4 == 3:
                        mm.then_inc(s_xt, 1)

            def step1(k, v, easy, b):
                g, u = SLOTS * k + v, v % 2
                if isinstance(g, int) and g == 0:
                    transposes(0, 0)
                if not (isinstance(g, int) and g >= NG - 2):
                    transposes(k + (v + 1) // SLOTS, (v + 1) % SLOTS)
                beside = ([] if b is None else [None, lambda: block1b(b)] if u == 0 else
                          [lambda: agg(b, 1, 2 * b + 3, b - 2), None, lambda: upd_in(b, 1, *place(b)), lambda: upd_out(b, 1, place(b)[0])])
                for j, also in enumerate(spaced(beside)):
                    if j == 0:
                        if isinstance(g, int) and g == 0:
                            pe.wait_ge(s_w1, W1_LANDED)
                            pe.wait_ge(s_bias, 1)
                        pe.wait_ge(s_edge[u], 16 * (2 * k + v // 2 + 1))
                    if j % 2 == 0:
                        pe.wait_ge(s_feat, 2 * g + j // 2 + 1)
                    wait(pe, s_gelu, 4 * g + j - 1)
                    nc.tensor.matmul(ps_hid[j % 2][:, 0:2 * HC], ones_b[:, :], flat(b1_split[:, :, :]), start=True, stop=False)
                    for q in range(2):
                        m = 2 * j + q
                        mm = nc.tensor.matmul(ps_hid[j % 2][:, HC * q:HC * (q + 1)], feat[u][:, P * m:P * (m + 1)], w1[:, :],
                                              start=False, stop=(q == 1))
                    mm.then_inc(s_pre, 1)
                    if also is not None:
                        also()
                    if u == 0 and j == 0 and not (isinstance(g, int) and g == 0):
                        window1(g - 2, 0, easy)
                    if isinstance(g, int) and g == NG - 2 and j == 1:
                        transposes(k, v + 1)
                if u == 0 and not (isinstance(g, int) and g == 0):
                    window1(g - 1, 1, easy)

            def place(b):
                if isinstance(b, int) and b > NB - LAST:
                    return b - (NB - LAST), NB - LAST
                return 0, b

            def agg(b, n, added, copied):
                pe.wait_ge(s_acc, added)
                if isinstance(b, int) and b == 0:
                    pe.wait_ge(s_wts, WTS_LANDED)
                    pe.wait_ge(s_nodes, 32)
                    pe.wait_ge(s_fill, 1)
                wait(pe, s_xstc, copied)
                nc.tensor.matmul(ps_bt[0:ND, 0:P * n], mw2[:, :], acc1[0:ND + 1, ds(P * b, P * n)],
                                 start=True, stop=True).then_inc(s_agg, n)

            def upd_in(b, n, slot, read):
                pe.wait_ge(s_aggc, b + n)
                nc.tensor.matmul(ps_bt[0:ND, P * n:2 * P * n], uw1x[:, :], x_t[:, ds(P * b, P * n)], start=True, stop=False)
                nc.tensor.matmul(ps_bt[0:ND, P * n:2 * P * n], uw1a[:, :], agg_t[:, 0:P * n],
                                 start=False, stop=True).then_inc(s_upre, n)
                wait(pe, s_updr, read)
                pe.wait_ge(s_wsum, b + n)
                for m in range(n):
                    nc.tensor.matmul(ps_bn[:, VC * (slot + m) + ND:VC * (slot + m) + ND + 1], wsum[ND:VC, P * m:P * (m + 1)],
                                     pick_w[ND:VC, :], start=True, stop=True)

            def upd_out(b, n, slot):
                pe.wait_ge(s_ugelu, b + n)
                for m in range(n):
                    nc.tensor.matmul(ps_bn[:, VC * (slot + m):VC * (slot + m) + ND], upd_t[:, P * m:P * (m + 1)], uw2[:, :],
                                     start=True, stop=True).then_inc(s_upd, 1)

            def block1a(b):
                agg(b, 1, NG, b - 1)
                upd_in(b, 1, 0, b)
                upd_out(b, 1, 0)

            def close1():
                window1(NG - 2, 0, False)
                window1(NG - 1, 1, False)

            def end1():
                window1(NG - 2, 0, True)
                window1(NG - 1, 1, True)
                agg(NB - 2, 2, NG, NB - LAST - 1)
                upd_in(NB - 2, 2, *place(NB - 2))
                upd_out(NB - 2, 2, place(NB - 2)[0])
                block1b(NB - LAST - 1)
                pe.wait_ge(s_xstc, NB - LAST)
                pe.wait_ge(s_xs, NB)
                for m in range(LAST):
                    nc.tensor.transpose(ps_bt[0:ND, P * m:P * (m + 1)], xs[:, m, :], ident[:, :]).then_inc(s_xst, 1)

            def block1b(b):
                wait(pe, s_xstc, b)
                pe.wait_ge(s_xs, b + 1)
                nc.tensor.transpose(ps_bt[0:ND, 2 * P:3 * P], xs[:, 0, :], ident[:, :]).then_inc(s_xst, 1)

            run_pass(pe, step1, block1a, block1b, ahead=True, even=LAG + 3, odd=LAG, end=end1, close=close1)

            def step2(k, v, easy, b):
                g, u = SLOTS * k + v, v % 2
                last = isinstance(b, int) and b == NB - 1 - LAG
                if last:
                    block2(b)
                pe.wait_ge(s_rows2[v], group_rows(k, v))
                pe.wait_ge(s_hot2, g + 1)
                window(g, u, easy, rows[v], ND, s_acc2, s_win2[u], s_far_hot2, s_far_win2)
                if b is not None and not last:
                    block2(b)

            def block2(b, n=1):
                pe.wait_ge(s_sum2, b + n)
                wait(pe, s_finr, b)
                for m in range(n):
                    nc.tensor.matmul(ps_bn[:, VC * m:VC * m + ND], agg_t[:, P * m:P * (m + 1)], w_gcn[:, :],
                                     start=True, stop=True).then_inc(s_fin, 1)

            def end2():
                block2(NB - 2, 2)
            run_pass(pe, step2, block2, odd=LAG, end=end2)

        @block.scalar
        def _(act):
            def copy_rows(g, u):
                for m in range(2):
                    act.wait_ge(s_xt, 2 * g + m + 1)
                    nc.scalar.activation(feat[u][0:ND, 4 * P * m:4 * P * (m + 1)], ps_xt[m][0:ND, :], ACT.Copy).then_inc(s_feat, 1)

            def step1(k, v, easy, b):
                g, u = SLOTS * k + v, v % 2
                if isinstance(g, int) and g == 0:
                    copy_rows(0, 0)
                if not (isinstance(g, int) and g >= NG - 2):
                    copy_rows(g + 1, 1 - u)
                wait(act, s_vals, g - 1)
                beside = ([] if b is None else [None, lambda: block1b(b)] if u == 0 else
                          [lambda: copy_sums(b, 1), None, lambda: upd_gelu(b, 1)])
                for j, also in enumerate(spaced(beside)):
                    act.wait_ge(s_pre, 4 * g + j + 1)
                    nc.scalar.activation(flat(hid[u][:, 2 * j:2 * j + 2, :]), ps_hid[j % 2][:, 0:2 * HC], ACT.Gelu).then_inc(s_gelu, 1)
                    if j == (0 if isinstance(g, int) and g == NG - 1 else SQUASH_AFTER[u]) and not (isinstance(g, int) and g == 0):
                        squash1(g - 1, 1 - u)
                    if isinstance(g, int) and g == NG - 2 and j == 1:
                        copy_rows(g + 1, 1 - u)
                    if also is not None:
                        also()
                if not (isinstance(g, int) and g >= NG - 2):
                    act.dma_start(feat[u][ND:P, :], edge_view[:, ds(g + 2, 1), :].rearrange("p o c -> p (o c)")).then_inc(s_edge[u], 16)

            def squash1(g, u):
                act.wait_ge(s_logit, g + 1)
                nc.scalar.activation(squash[u][:, :], logit[u][:, :], ACT.Tanh, bias=half_gb2[:, :], scale=0.5).then_inc(s_squash, 1)

            def copy_sums(b, n):
                wait(act, s_upd, b)
                act.wait_ge(s_agg, b + n)
                nc.scalar.activation(agg_t[:, 0:P * n], ps_bt[0:ND, 0:P * n], ACT.Copy).then_inc(s_aggc, n)
                nc.scalar.activation(wsum[ND:VC, 0:P * n], acc1[ND:VC, ds(P * b, P * n)], ACT.Copy).then_inc(s_wsum, n)

            def upd_gelu(b, n):
                act.wait_ge(s_upre, b + n)
                nc.scalar.activation(upd_t[0:ND, 0:P * n], ps_bt[0:ND, P * n:2 * P * n], ACT.Gelu).then_inc(s_ugelu, n)

            def block1a(b):
                copy_sums(b, 1)
                upd_gelu(b, 1)

            def close1():
                squash1(NG - 1, 1)

            def end1():
                squash1(NG - 1, 1)
                copy_sums(NB - 2, 2)
                upd_gelu(NB - 2, 2)
                block1b(NB - LAST - 1)
                for m in range(0, LAST, 2):
                    act.wait_ge(s_xs, NB - LAST + m + 1)
                    act.dma_start(x1s_view[:, NB - LAST + m, :], xs[:, m, :]).then_inc(s_xsw, 16)
                act.wait_ge(s_xst, NB)
                nc.scalar.activation(acc2[:, P * (NB - LAST):P * NB], ps_bt[0:ND, 0:P * LAST], ACT.Copy).then_inc(s_xstc, LAST)

            def block1b(b):
                b = at(act, b)
                act.wait_ge(s_xs, b + 1)
                act.dma_start(x1s_view[:, ds(b, 1), :], xs[:, 0:1, :]).then_inc(s_xsw, 16)
                act.wait_ge(s_xst, b + 1)
                nc.scalar.activation(acc2[:, ds(P * b, P)], ps_bt[0:ND, 2 * P:3 * P], ACT.Copy).then_inc(s_xstc, 1)
            run_pass(act, step1, block1a, block1b, ahead=True, even=LAG + 3, odd=LAG, end=end1, close=close1)

            def step2(k, v, easy, b):
                if b is not None and v % 2:
                    block2(b, 2 * b + 3)
                elif b is not None:
                    block2b(b)

            def block2(b, added, n=1):
                act.wait_ge(s_acc2, added)
                wait(act, s_fin, b)
                nc.scalar.activation(agg_t[:, 0:P * n], acc2[:, ds(P * b, P * n)], ACT.Copy).then_inc(s_sum2, n)

            def end2():
                block2b(NB - 3)
                block2(NB - 2, NG, 2)
                block2b(NB - 2)

            def block2b(b):
                b = at(act, b)
                act.wait_ge(s_y, b + 1)
                act.dma_start(out_view[:, ds(b, 1), :], y[:, 0:1, :]).then_inc(s_out, 16)
            run_pass(act, step2, lambda b: block2(b, NG), block2b, even=LAG + 1, odd=LAG, end=end2)
            act.wait_ge(s_out, 16 * NB)

        @block.vector
        def _(dve):
            nc.vector.memset(b1_split[:, :, :], 0.0)
            nc.vector.memset(acc2[:, NP:AW], 0.0)
            nc.vector.memset(rin[:, :], 1.0)
            nc.vector.memset(upd_t[ND:ND + 1, :], 1.0).then_inc(s_fill, 1)

            chain = [0]

            def link(ins):
                chain[0] += 1
                ins.then_inc(s_chain, 1)
                dve.wait_ge(s_chain, chain[0])

            dve.wait_ge(s_win_in, 16)
            nc.vector.tensor_reduce(lo[:, :], dst_rows[:, :], AX, ALU.min)
            link(nc.vector.tensor_reduce(hi[:, :], dst_rows[:, :], AX, ALU.max))
            link(nc.vector.tensor_tensor(reach[:, :], hi[:, :], lo[:, :], ALU.subtract))
            dve.wait_ge(s_const, N_CONST)
            nc.vector.tensor_copy(iota_w[:, :], iota_i[:, :])
            nc.vector.tensor_copy(due[:, :], due_i[:, :])
            link(nc.vector.tensor_copy(win_off[:, :], win_i[:, :]))
            link(nc.vector.tensor_scalar(crossed[:, 1:NW], win_off[0:NG, 1:NW], reach[:, :], None, ALU.is_le))
            link(nc.vector.tensor_reduce(extra[:, :], crossed[:, 1:NW], AX, ALU.add))
            nc.vector.tensor_scalar(spread[:, 0:NG], ident[0:NG, 0:NG], lo[:, :], None, ALU.mult)
            nc.vector.tensor_scalar(spread[:, NG:2 * NG], ident[0:NG, 0:NG], extra[:, :], None, ALU.mult)
            nc.vector.scalar_tensor_tensor(spread[:, 3 * NG:3 * NG + 1], lo[:, :], due[0:NG, :], extra[:, :],
                                           ALU.is_lt, ALU.add)
            nc.vector.tensor_scalar(spread[:, 2 * NG:3 * NG], before[0:NG, :], extra[:, :], None, ALU.mult).then_inc(s_spread, 1)
            dve.wait_ge(s_bcast, 1)
            nc.vector.tensor_copy(steer[0:1, :], ps_bn[0:1, 0:3 * NG + 1])
            link(nc.vector.tensor_copy(lo_all[:, :], ps_bn[:, 0:NG]))
            dve.wait_ge(s_dst, 32)
            link(nc.vector.tensor_tensor(dst_rel[:, :].rearrange("p (g k) -> p g k", k=TG),
                                         dst_i[:, :].rearrange("p (g k) -> p g k", k=TG),
                                         lo_all[:, :].rearrange("p (g o) -> p g o", o=1).to_broadcast([P, NG, TG]),
                                         ALU.subtract))
            dve.wait_ge(s_w1, W1_LANDED)
            rest = b1
            for k in range(3):
                link(nc.vector.tensor_copy(b1_hi[:, :, :], rest[:, :, :]))
                link(nc.vector.tensor_scalar(b1_part[:, :, :], b1_hi[:, :, :], ident[0:3, k:k + 1], None, ALU.mult))
                if k == 0:
                    link(nc.vector.tensor_copy(b1_sum[:, :, :], b1_part[:, :, :]))
                else:
                    link(nc.vector.tensor_tensor(b1_sum[:, :, :], b1_sum[:, :, :], b1_part[:, :, :], ALU.add))
                link(nc.vector.tensor_tensor(b1_rest[:, :, :], rest[:, :, :], b1_hi[:, :, :], ALU.subtract))
                rest = b1_rest
            link(nc.vector.tensor_copy(b1_split[0:3, :, :], b1_sum[:, :, :]))
            nc.vector.memset(step[:, 0:1], 0.0).then_inc(s_bias, 1)
            dve.wait_ge(s_wts, WTS_LANDED)
            link(nc.vector.tensor_scalar(half_gb2[:, :], gb2[:, :], 0.5, None, ALU.mult))
            nc.vector.memset(step[:, 1:2], 0.0).then_inc(s_steer, 1)
            nc.vector.memset(acc1[:, :], 0.0)

            def over_window(ap):
                return ap.rearrange("p (k o) -> p k o", o=1).to_broadcast([P, TG, W])

            def one_hot(place, rel):
                return nc.vector.tensor_tensor(
                    place[:, :, :], over_window(rel),
                    iota_w[:, :].rearrange("p (o w) -> p o w", o=1).to_broadcast([P, TG, W]), ALU.is_equal)

            def weigh_hot(place, g):
                return nc.vector.tensor_tensor(place[:, :, :], place[:, :, :], over_window(weight[:, ds(TG * g, TG)]), ALU.mult)

            def take_window(acc, rws, g, u, easy, win_sem, win_count, acc_sem, far_hot_sem, far_win_sem, weigh):
                first_node = dve.value_load(steer[0:1, ds(g, 1)], min_val=0, max_val=NP - 1)
                nc.vector.drain()
                dve.wait_ge(win_sem, win_count)
                added = nc.vector.tensor_tensor(acc[0:rws, ds(first_node, W)], acc[0:rws, ds(first_node, W)],
                                                ps_win[u][0:rws, 0:W], ALU.add)
                if easy:
                    added.then_inc(acc_sem, 1)
                    return
                more = dve.value_load(steer[0:1, ds(NG + g, 1)], min_val=0, max_val=NW - 1)
                with dve.If(more > 0):
                    done = dve.value_load(steer[0:1, ds(2 * NG + g, 1)], min_val=0, max_val=NW * NG)
                    with dve.Fori(1, more + 1) as w:
                        nc.vector.drain()
                        nc.vector.tensor_scalar(far_rel[:, :], dst_rel[:, ds(TG * g, TG)], win_off[:, ds(w, 1)], None,
                                                ALU.subtract)
                        nc.vector.drain()
                        if weigh:
                            one_hot(far_hot, far_rel[:, :])
                            nc.vector.drain()
                            weigh_hot(far_hot, g).then_inc(far_hot_sem, 1)
                        else:
                            one_hot(far_hot, far_rel[:, :]).then_inc(far_hot_sem, 1)
                        dve.wait_ge(far_win_sem, done + w)
                        node = nc.s_assert_within(dve.snap(first_node + w * W), 0, AW - W)
                        nc.vector.tensor_tensor(acc[0:rws, ds(node, W)], acc[0:rws, ds(node, W)],
                                                ps_win[u][0:rws, 0:W], ALU.add)
                nc.vector.drain()
                nc.vector.memset(far_rel[:, 0:1], 0.0).then_inc(acc_sem, 1)

            def rsqrt(n):
                v, r, s = rin[:, 0:n], root[:, 0:n], step[:, 0:n]
                nc.vector.drain()
                nc.vector.tensor_scalar(s.bitcast(i32), v.bitcast(i32), 1, None, ALU.logical_shift_right)
                nc.vector.drain()
                nc.vector.tensor_scalar(r.bitcast(i32), s.bitcast(i32), -1.0, ROOT_SEED, ALU.mult, ALU.add)
                for _ in range(3):
                    nc.vector.drain()
                    nc.vector.scalar_tensor_tensor(s, r, -0.5, r, ALU.mult, ALU.mult)
                    nc.vector.drain()
                    nc.vector.tensor_tensor(s, s, v, ALU.mult)
                    nc.vector.drain()
                    nc.vector.scalar_tensor_tensor(r, s, 1.5, r, ALU.add, ALU.mult)
                nc.vector.drain()

            def window1(g, u, easy):
                take_window(acc1, VC, g, u, easy, s_win, g + 1, s_acc, s_far_hot, s_far_win, False)

            def gate1(g, u):
                dve.wait_ge(s_squash, g + 1)
                nc.vector.tensor_scalar(vals[u][:, :, ND:ND + 1], squash[u][:, :].rearrange("p (k o) -> p k o", o=1),
                                        0.5, 0.5, ALU.mult, ALU.add)
                nc.vector.drain()
                nc.vector.tensor_tensor(vals[u][:, :, 0:ND], hid[u][:, :, 0:ND],
                                        vals[u][:, :, ND:ND + 1].to_broadcast([P, TG, ND]), ALU.mult).then_inc(s_vals, 1)

            def step1(k, v, easy, b):
                g, u = SLOTS * k + v, v % 2
                if u == 0 and not (isinstance(g, int) and g == 0):
                    gate1(g - 1, 1)
                if not (isinstance(g, int) and g < 2):
                    window1(g - 2, u, easy)
                one_hot(hot[u], dst_rel[:, ds(TG * g, TG)])
                nc.vector.tensor_copy(vals[u][:, :, ND + 1:VC], weight[:, ds(TG * g, TG)].rearrange("p (k o) -> p k o", o=1))
                if u == 1:
                    gate1(g - 1, 0)
                if b is not None and not (isinstance(b, int) and b == NB - LAST):
                    block1a(b)
                dve.wait_ge(s_gelu, 4 * g + 4)
                nc.vector.tensor_tensor(prod[:, :, :], hid[u][:, :, ND:HC],
                                        gw2[:, :].rearrange("p (o c) -> p o c", o=1).to_broadcast([P, TG, ND]), ALU.mult)
                nc.vector.drain()
                nc.vector.tensor_reduce(logit[u][:, :], prod[:, :, :], AX, ALU.add).then_inc(s_logit, 1)

            def close1(easy=False):
                gate1(NG - 1, 1)
                window1(NG - 2, 0, easy)
                window1(NG - 1, 1, easy)

            def block1(firsts, seconds):
                row = lambda a, b: a[:, ds(b, 1), :].rearrange("p o c -> p (o c)")
                column = lambda a: a.rearrange("p (m o) -> p m o", o=1)
                n_a, n_b = len(firsts), len(seconds)
                n = n_a + n_b
                nc.vector.drain()
                for m in range(n_b):
                    nc.vector.bn_stats(stats[:, n_a + m, :], h2[:, m, :])
                if n_a:
                    these = ds(firsts[0], n_a)
                    if isinstance(firsts[0], int) and firsts[0] == 0:
                        dve.wait_ge(s_nodes, 32)
                    dve.wait_ge(s_upd, firsts[-1] + 1)
                    sums = ps_bn[:, 0:VC * n_a].rearrange("p (m c) -> p m c", c=VC)
                    nc.vector.tensor_tensor(h[:, 0:n_a, :], x_nat[:, these, :], sums[:, :, 0:ND], ALU.add)
                    nc.vector.tensor_scalar(column(deg[:, 0:n_a]), sums[:, :, ND:ND + 1], 1.0, 0.0, ALU.add, ALU.is_gt)
                    nc.vector.tensor_scalar(column(rin[:, n:n + n_a]), sums[:, :, ND:ND + 1], 1.0, 1e-30, ALU.add,
                                            ALU.max).then_inc(s_updr, n_a)
                    nc.vector.tensor_tensor(x1b[:, these, :], x_nat[:, these, :],
                                            ln_b[:, :].rearrange("p (o c) -> p o c", o=1).to_broadcast([P, n_a, ND]), ALU.add)
                nc.vector.drain()
                for m in range(n_a):
                    nc.vector.bn_stats(stats[:, m, :], h[:, m, :])
                nc.vector.drain()
                for m in range(n):
                    nc.vector.bn_aggr(mv[:, m, :], stats[:, m, :])
                nc.vector.drain()
                nc.vector.tensor_scalar(column(rin[:, 0:n]), mv[:, 0:n, 1:2], EPS, None, ALU.add)
                for m in range(n_a):
                    nc.vector.scalar_tensor_tensor(h_g[:, m, :], h[:, m, :], mv[:, m, 0:1], ln_g[:, :], ALU.subtract, ALU.mult)
                for m in range(n_b):
                    nc.vector.tensor_scalar(h2_c[:, m, :], h2[:, m, :], mv[:, n_a + m, 0:1], None, ALU.subtract)
                rsqrt(n + n_a)
                for m, b in enumerate(seconds):
                    root_b = root[:, n_a + m:n_a + m + 1]
                    if m == 0:
                        wait(dve, s_xst, b)
                        wait(dve, s_xsw, 16 * b)
                    nc.vector.tensor_scalar(xs[:, m, :], h2_c[:, m, :], root_b, dinv[:, ds(b, 1)], ALU.mult,
                                            ALU.mult).then_inc(s_xs, 1)
                for m, b in enumerate(seconds):
                    root_b = root[:, n_a + m:n_a + m + 1]
                    nc.vector.scalar_tensor_tensor(row(x1b, b), h2_c[:, m, :], root_b, b_gcn[:, :], ALU.mult, ALU.add)
                if n_a:
                    nc.vector.tensor_tensor(dinv[:, these], root[:, n:n + n_a], deg[:, 0:n_a], ALU.mult)
                for m, b in enumerate(firsts):
                    nc.vector.scalar_tensor_tensor(h2[:, m, :], h_g[:, m, :], root[:, m:m + 1], row(x1b, b), ALU.mult, ALU.add)

            def block1a(b):
                block1([b], [] if isinstance(b, int) and b == 0 else [b - 1])

            def finish1():
                block1([], [NB - 1])

            def end1():
                close1(True)
                last = list(range(NB - LAST, NB))
                block1(last, [NB - LAST - 1])
                block1([], last)
            run_pass(dve, step1, block1a, ahead=True, even=LAG + 1, end=end1, close=close1, finish=finish1)
            dve.wait_ge(s_xstc, NB)

            def step2(k, v, easy, b):
                g, u = SLOTS * k + v, v % 2
                one_hot(hot[u], dst_rel[:, ds(TG * g, TG)])
                nc.vector.drain()
                weigh_hot(hot[u], g).then_inc(s_hot2, 1)
                if not (isinstance(g, int) and g == 0):
                    take_window(acc2, ND, g - 1, 1 - u, easy, s_win2[1 - u], 2 * k + v // 2 + u, s_acc2, s_far_hot2, s_far_win2, True)
                if b is not None:
                    block2([b])

            def close2(easy=False):
                take_window(acc2, ND, NG - 1, 1, easy, s_win2[1], TURNS, s_acc2, s_far_hot2, s_far_win2, True)

            def block2(blocks):
                n = len(blocks)
                nc.vector.drain()
                for m, b in enumerate(blocks):
                    if m == 0:
                        dve.wait_ge(s_fin, blocks[-1] + 1)
                    nc.vector.scalar_tensor_tensor(h[:, m, :], ps_bn[:, VC * m:VC * m + ND], dinv[:, ds(b, 1)],
                                                   x1b[:, ds(b, 1), :].rearrange("p o c -> p (o c)"),
                                                   ALU.mult, ALU.add).then_inc(s_finr, 1)
                nc.vector.drain()
                for m in range(n):
                    nc.vector.bn_stats(stats[:, m, :], h[:, m, :])
                nc.vector.drain()
                for m in range(n):
                    nc.vector.bn_aggr(mv[:, m, :], stats[:, m, :])
                nc.vector.drain()
                nc.vector.tensor_scalar(rin[:, 0:n].rearrange("p (k o) -> p k o", o=1), mv[:, 0:n, 1:2], EPS, None, ALU.add)
                rsqrt(n)
                wait(dve, s_out, 16 * blocks[0])
                for m in range(n):
                    nc.vector.tensor_scalar(y[:, m, :], h[:, m, :], mv[:, m, 0:1], root[:, m:m + 1], ALU.subtract,
                                            ALU.mult).then_inc(s_y, 1)

            def end2():
                close2(True)
                block2([NB - 2, NB - 1])
            run_pass(dve, step2, lambda b: block2([b]), odd=LAG, end=end2, close=close2)



def kernel(**inputs):
    import numpy as np
    import concourse.bacc as bacc
    from concourse import mybir as mb
    from concourse.bass_utils import run_bass_kernel_spmd

    a = {k.replace("L0_gnn_", "").replace("L1_gnn_", ""): np.asarray(v) for k, v in inputs.items()}
    EPAD = NT * P

    def by_tile(v, fill):
        full = np.full((EPAD,), fill, v.dtype)
        full[:E] = v
        return full.reshape(NT, P).T

    x = np.zeros((NP, ND), np.float32)
    x[:N] = a["x"]
    edge = np.zeros((EPAD, ED), np.float32)
    edge[:E] = a["edge_attr_32"]
    dst = np.full((EPAD,), N, np.int32)
    dst[:E] = a["dst"]
    rep = lambda v, n=P: np.broadcast_to(v.reshape(1, -1), (n, v.size))
    arrays = {
        "x_t": np.concatenate([x.T, np.ones((1, NP), np.float32)]),
        "x_nat": x,
        "src_t": by_tile(a["src"].astype(np.int32), 0),
        "dst_t": by_tile(a["dst"].astype(np.int32), N),
        "dst_rows": dst.reshape(NG, GE),
        "weight_t": by_tile(a["edge_weight"], 0),
        "edge_t": edge.T,
        "mW1": a["mW1"], "gW1": a["gW1"], "mb1_3": rep(a["mb1"], 3), "gb1_3": rep(a["gb1"], 3),
        "gW2": rep(a["gW2"]), "gb2": rep(a["gb2"]),
        "mW2": a["mW2"], "mb2": a["mb2"].reshape(1, ND),
        "uW1": a["uW1"], "ub1": a["ub1"].reshape(1, ND), "uW2": a["uW2"], "ub2": a["ub2"].reshape(1, ND),
        "W": a["W"], "ln_g": rep(a["ln_g"]), "ln_b": rep(a["ln_b"]), "b": rep(a["b"]),
    }
    arrays = {f"in_{k}": np.ascontiguousarray(v) for k, v in arrays.items()}
    nc = bacc.Bacc("TRN2", target_bir_lowering=False, num_devices=1)
    t = {k[3:]: nc.dram_tensor(k, v.shape, mb.dt.from_np(v.dtype), kind="ExternalInput").ap() for k, v in arrays.items()}
    out = nc.dram_tensor("out_nodes", (NP, ND), mb.dt.float32, kind="ExternalOutput").ap()
    gnn_kernel(nc, t, out)
    r = run_bass_kernel_spmd(nc, [arrays], core_ids=[0])
    return r.results[0]["out_nodes"][:N]
```
